# Optimizing a Trainium2 kernel written in Bass

```python
import numpy as np
import jax
import jax.numpy as jnp

def _softmax(x, axis=-1):
    return jax.nn.softmax(x, axis=axis)

def _gelu(x):
    return jax.nn.gelu(x, approximate=True)

def _silu(x):
    return jax.nn.silu(x)

def _sigmoid(x):
    return jax.nn.sigmoid(x)

def _layernorm(x, axis=-1, eps=1e-05):
    m = jnp.mean(x, axis=axis, keepdims=True)
    v = jnp.var(x, axis=axis, keepdims=True)
    return (x - m) / jnp.sqrt(v + eps)

def _scatter_add(tgt, idx, src, axis=0):
    return tgt.at[idx].add(src)

def _segment_sum(src, seg, n):
    return jax.ops.segment_sum(src, seg, n)
kernel_name = 'mk_seq_postln_d1_jaxref_r8_489696'

def setup_inputs(seed: int=0):
    np.random.seed(seed)
    _w = jnp.asarray

    def _L0_attn_setup():
        import jax, jax.numpy as jnp
        import numpy as np
        import math
        D_MODEL = 128
        N_HEADS = 16
        DH = D_MODEL // N_HEADS
        THETA = 10000.0

        def _rope_tables(S):
            inv_freq = 1.0 / THETA ** (jnp.arange(0, DH, 2, dtype=jnp.float32) / DH)
            ang = jnp.arange(S, dtype=jnp.float32)[:, None] * inv_freq[None, :]
            cos = jnp.concatenate([jnp.cos(ang), jnp.cos(ang)], axis=-1)
            sin = jnp.concatenate([jnp.sin(ang), jnp.sin(ang)], axis=-1)
            return (cos, sin)

        def _apply_rope(x, cos, sin):
            x1, x2 = jnp.split(x, 2, axis=-1)
            rot = jnp.concatenate([-x2, x1], axis=-1)
            c = cos[None, :, None, :]
            s = sin[None, :, None, :]
            return x * c + rot * s
        key = jax.random.key(seed)
        k1, k2, k3 = jax.random.split(key, 3)
        x = jax.random.normal(k1, (4, 256, D_MODEL), dtype=jnp.float32)
        qkv = 0.01 * jax.random.normal(k2, (3 * D_MODEL, D_MODEL), dtype=jnp.float32)
        wo = 0.01 * jax.random.normal(k3, (D_MODEL, D_MODEL), dtype=jnp.float32)
        return {'x': x, 'qkv': qkv, 'wo': wo}
    _L0_attn_in = _L0_attn_setup()

    def _L0_ffn_setup():
        import jax, jax.numpy as jnp
        import numpy as np
        DIM = 128
        HIDDEN = 384
        SCALE = 1.0 / 127.0

        def _dequant(w_int, dtype):
            return w_int.astype(dtype) * jnp.asarray(SCALE, dtype)
        key = jax.random.key(seed)
        k_x, k_g, k_u, k_d = jax.random.split(key, 4)
        x = jax.random.normal(k_x, (4, 256, DIM), dtype=jnp.float32)
        w_gate = jax.random.randint(k_g, (HIDDEN, DIM), -127, 128, dtype=jnp.int32)
        w_up = jax.random.randint(k_u, (HIDDEN, DIM), -127, 128, dtype=jnp.int32)
        w_down = jax.random.randint(k_d, (DIM, HIDDEN), -127, 128, dtype=jnp.int32)
        return {'x': x, 'w_gate': w_gate, 'w_up': w_up, 'w_down': w_down}
    _L0_ffn_in = _L0_ffn_setup()
    _d = {'L0_attn_x': _L0_attn_in['x'], 'L0_attn_qkv': _L0_attn_in['qkv'], 'L0_attn_wo': _L0_attn_in['wo'], 'L0_ffn_w_gate': _L0_ffn_in['w_gate'], 'L0_ffn_w_up': _L0_ffn_in['w_up'], 'L0_ffn_w_down': _L0_ffn_in['w_down']}
    _x0 = _d['L0_attn_x']
    _d['L0_attn_x'] = jax.random.normal(jax.random.fold_in(jax.random.key(seed), 1), (2, 1024, 128), dtype=_x0.dtype)
    del _x0
    return _d

def reference(L0_attn_x, L0_attn_qkv, L0_attn_wo, L0_ffn_w_gate, L0_ffn_w_up, L0_ffn_w_down):

    def _L0_attn_ref(x, qkv, wo):
        import jax, jax.numpy as jnp
        import numpy as np
        import math
        D_MODEL = 128
        N_HEADS = 16
        DH = D_MODEL // N_HEADS
        THETA = 10000.0

        def _rope_tables(S):
            inv_freq = 1.0 / THETA ** (jnp.arange(0, DH, 2, dtype=jnp.float32) / DH)
            ang = jnp.arange(S, dtype=jnp.float32)[:, None] * inv_freq[None, :]
            cos = jnp.concatenate([jnp.cos(ang), jnp.cos(ang)], axis=-1)
            sin = jnp.concatenate([jnp.sin(ang), jnp.sin(ang)], axis=-1)
            return (cos, sin)

        def _apply_rope(x, cos, sin):
            x1, x2 = jnp.split(x, 2, axis=-1)
            rot = jnp.concatenate([-x2, x1], axis=-1)
            c = cos[None, :, None, :]
            s = sin[None, :, None, :]
            return x * c + rot * s
        B, S, D = x.shape
        QKV = x @ qkv.T
        Q, K, V = jnp.split(QKV, 3, axis=-1)
        q = Q.reshape(B, S, N_HEADS, DH)
        k = K.reshape(B, S, N_HEADS, DH)
        v = V.reshape(B, S, N_HEADS, DH)
        cos, sin = _rope_tables(S)
        q = _apply_rope(q, cos, sin)
        k = _apply_rope(k, cos, sin)
        q = q.transpose(0, 2, 1, 3)
        k = k.transpose(0, 2, 1, 3)
        v = v.transpose(0, 2, 1, 3)
        scores = jnp.einsum('bhsd,bhtd->bhst', q, k) / math.sqrt(float(DH))
        mask = jnp.tril(jnp.ones((S, S), dtype=scores.dtype))
        scores = scores * mask
        scores = jnp.where(scores == 0.0, -jnp.inf, scores)
        attn = jax.nn.softmax(scores, axis=-1)
        out = jnp.einsum('bhst,bhtd->bhsd', attn, v)
        out = out.transpose(0, 2, 1, 3).reshape(B, S, D)
        return out @ wo.T

    def _L0_ffn_ref(x, w_gate, w_up, w_down):
        import jax, jax.numpy as jnp
        import numpy as np
        DIM = 128
        HIDDEN = 384
        SCALE = 1.0 / 127.0

        def _dequant(w_int, dtype):
            return w_int.astype(dtype) * jnp.asarray(SCALE, dtype)
        wg = _dequant(w_gate, x.dtype)
        wu = _dequant(w_up, x.dtype)
        wd = _dequant(w_down, x.dtype)
        gate = jnp.einsum('bsd,hd->bsh', x, wg)
        up = jnp.einsum('bsd,hd->bsh', x, wu)
        h = jax.nn.silu(gate) * up
        return jnp.einsum('bsh,dh->bsd', h, wd)
    x = L0_attn_x
    x = _layernorm(x + _L0_attn_ref(x, L0_attn_qkv, L0_attn_wo), axis=-1)
    x = _layernorm(x + _L0_ffn_ref(x, L0_ffn_w_gate, L0_ffn_w_up, L0_ffn_w_down), axis=-1)
    return x

_drawn_inputs = setup_inputs


def setup_inputs(seed=0):
    import zlib

    import numpy as np

    out = dict(_drawn_inputs(seed))
    spreads = {}
    factors = {'L0_attn_qkv': 8.0, 'L0_attn_wo': 8.0}
    for name, (base, spread) in spreads.items():
        noise = np.random.default_rng([zlib.crc32(name.encode()), seed]).standard_normal(out[name].shape)
        drawn = base * np.exp(spread * noise) if base else spread * noise
        out[name] = jnp.asarray(drawn.astype(out[name].dtype))
    for name, factor in factors.items():
        out[name] = (out[name] * factor).astype(out[name].dtype)
    return out
```

```python
from contextlib import ExitStack

import concourse.bass as bass
from concourse import mybir

F32 = mybir.dt.float32
BF16 = mybir.dt.bfloat16
I32 = mybir.dt.int32
ALU = mybir.AluOpType
ACT = mybir.ActivationFunctionType
AX_X, AX_XYZ = mybir.AxisListType.X, mybir.AxisListType.XYZ

P = 128
B, S, D = 2, 1024, 128
HEADS, DH = 16, 8
HID = 384
NHC = HID // P
C = 512
CT = C // P
HALVES = S // C
NCH = B * HALVES
NT = S // P
SCORE_SCALE = float(DH) ** -0.5
DEQUANT = 1.0 / 127.0
EPS = 1e-5
WINDOW, V_LIMIT = 1e20, 1e12
RING = 3
NP = 8
LAG = 4
SETS, GROUPS = 2, 2
SH = HEADS // SETS
TERMS = 9
ROWS = TERMS * DH


def group_units(half):
    units = []
    first = half * CT
    for i in range(first):
        for jp in range(2):
            units.append(([(jp, jl, i, 0, C, 0) for jl in range(2)], None, [i] if jp else []))
    for jp in range(2):
        units.append(([(jp, jl, first, 0, C, 0) for jl in range(2)], "first", [first] if jp else []))
    for jp in range(2):
        pieces = []
        for jl in range(2):
            pieces += [(jp, jl, first + 1, 0, 3 * P, P), (jp, jl, first + 3, 3 * P, P, 3 * P)]
        units.append((pieces, "outer", [first + 1, first + 3] if jp else []))
    units.append(([(jp, jl, first + 2, 2 * P * jp, 2 * P, 2 * P) for jp in range(2) for jl in range(2)],
                  "inner", [first + 2]))
    return units


def make_plan():
    def attend(b, half):
        units = group_units(half)
        return [("score", b, half, st, g, n, n == len(units) - 1 and g == 1)
                for st in range(SETS) for g in range(GROUPS) for n in range(len(units))]

    def prepare(c, at=0, step=1):
        items = [(at, ("xT", c)), (at + 1, ("q", c)), (at + 3, ("k", c)), (at + 5, ("v", c))]
        if c:
            items += [(at + 2 + step * i, ("rotate", c, i // 8, i % 8)) for i in range(16)]
        return items

    def finish(e, at):
        kinds = [("oT", e, 0), ("oT", e, 1), ("onT", e), ("proj", e), ("stats", e, 0), ("scale", e, 0), ("x1T", e),
                 ("gate", e, 0), ("up", e, 0), ("gate", e, 1), ("up", e, 1), ("gate", e, 2), ("up", e, 2),
                 ("down", e), ("stats", e, 1), ("scale", e, 1)]
        return list(zip(at, kinds))

    def weave(units, *extras):
        extra = sorted((x for xs in extras for x in xs), key=lambda x: x[0])
        out = []
        for i, u in enumerate(units):
            while extra and extra[0][0] <= i:
                out.append(extra.pop(0)[1])
            out.append(u)
        return out + [it for _, it in extra]

    plan = [("weights",)] + [it for _, it in prepare(0)[:4]] + [("load", 0), ("load", 1)]
    plan += weave(attend(0, 0), prepare(1, 1, 0.8))
    plan += weave(attend(0, 1), prepare(2, 0, 1.0), prepare(3, 18, 1.0),
                  [(25, ("ffnw", 0)), (26, ("ffnw", 1)), (27, ("ffnw", 2))],
                  finish(0, [28, 29, 30, 31, 32, 34, 36, 37, 38, 39, 41, 42, 44, 47, 48, 50]))
    plan += weave(attend(1, 1), finish(1, [7, 9, 11, 13, 14, 16, 19, 21, 23, 25, 27, 29, 31, 35, 36, 39]))
    plan += weave(attend(1, 0), finish(3, [6, 7, 8, 9, 10, 11, 12, 13, 14, 15, 16, 17, 18, 19.1, 19.2, 19.3]))
    out, due, seen, block = [], [], 0, 0
    total = sum(it[0] == "score" for it in plan)
    loads = []
    order = [(0, 0), (0, 1), (1, 1), (1, 0)]

    def split_for(k):
        b, half = order[k // 2]
        return all(("rotate", b * HALVES + h, 1, 7) in out for h in range(half + 1) if b or h)

    for it in plan:
        out.append(it)
        while loads and split_for(loads[0]):
            out.append(("load", loads.pop(0)))
        if it[0] != "score":
            continue
        due.append((seen + LAG, ("pv", seen)))
        if it[6]:
            if block + 2 < 2 * NCH:
                loads.append(block + 2)
            due.append((seen + LAG + 1, ("outputs", block)))
            block += 1
        while due and (due[0][0] <= seen or seen == total - 1):
            out.append(due.pop(0)[1])
        seen += 1
    last = [it for _, it in finish(2, [0] * 16)]
    return out + last[:3] + [("flag", None)] + last[3:]


def build(nc, x, qkv, wo, w_gate, w_up, w_down, cos_t, sin_t, out, stacks):
    plan = make_plan()
    tail = [it for it in plan if it[0] == "proj"][-1][1]
    slotted = [it for it in plan if it[0] in ("weights", "xT", "q", "k", "v", "ffnw", "score", "oT", "onT", "proj", "x1T",
                                              "flag", "gate", "up", "down")]
    side_items = [it for it in slotted if it[0] != "score" and not (it[0] in ("xT", "q", "k") and it[1] == 0)
                  and not (it[0] in ("oT", "onT", "proj", "x1T", "gate", "up", "down") and it[1] == tail)]
    scores = [it for it in plan if it[0] == "score"]
    units = {half: group_units(half) for half in range(HALVES)}
    blocks = []
    for it in scores:
        if it[1:4] not in blocks:
            blocks.append(it[1:4])
    finishing = [it[1] for it in plan if it[0] == "proj"]
    qk_items = [it for it in plan if it[0] in ("q", "k")]
    by_act = [it for it in slotted if it[0] in ("xT", "v", "ffnw", "onT", "x1T", "gate")
              or (it[0] == "up" and it[1] != tail)
              or (it[0] in ("q", "k") and it[1] > 0)]
    by_dve = [it for it in slotted if it[0] in ("weights", "oT", "proj", "down", "flag")]
    diagonal = [it for it in scores if units[it[2]][it[5]][1]]

    with ExitStack() as ctx:
        def sb(name, shape, dt=F32):
            return ctx.enter_context(nc.sbuf_tensor(name, shape, dt))

        def sem(name):
            return ctx.enter_context(nc.semaphore(name))

        slots = [ctx.enter_context(nc.psum_tensor(f"slot{i}", [P, 2, C], F32)) for i in range(RING)]
        o_acc = ctx.enter_context(nc.psum_tensor("o_acc", [P, C], F32))
        side = ctx.enter_context(nc.psum_tensor("side", [P, C], F32))

        ident = sb("ident", [P, P])
        x_sb = sb("x_sb", [P, B * NT, P])
        xT = sb("xT", [P, 2, C])
        w_qkv = sb("w_qkv", [P, 3, P])
        w_o = sb("w_o", [P, P])
        w_ffn_i = sb("w_ffn_i", [P, 3, HID], I32)
        w_ffn = w_ffn_i[:].bitcast(F32)
        wT = sb("wT", [P, 3, P])
        woT = sb("woT", [P, P])
        ffT = sb("ffT", [P, 3, HID])
        cos_sb = sb("cos_sb", [P, S])
        sin_sb = sb("sin_sb", [P, S])
        raw = sb("raw", [P, 2, C])
        rot = sb("rot", [P, 2, C])
        qk = sb("qk", [P, 2, C])
        parts = sb("parts", [P, 2, 3, C], BF16)
        qs = sb("qs", [ROWS, 2, SH, C], BF16)
        ks = sb("ks", [ROWS, SETS, HALVES, SH, C], BF16)
        vs = sb("vs", [P, B * NT, SETS * 4, GROUPS, 32])
        p_sb = sb("p_sb", [P, NP, 2, C])
        o_sb = sb("o_sb", [P, SETS, C])
        den_inv = sb("den_inv", [P, SETS, CT * 4, GROUPS])
        o_rows = sb("o_rows", [P, CT, SETS, 64])
        o_n = sb("o_n", [P, C])
        y = sb("y", [P, 2, CT, P])
        x1T = sb("x1T", [P, C])
        st6 = sb("st6", [P, CT, 6])
        mv = sb("mv", [P, CT, 2])
        minus_half = sb("minus_half", [P, CT])
        ve = sb("ve", [P, CT])
        rstd = sb("rstd", [P, CT])
        gu = sb("gu", [P, 2, 2, C])
        eg = sb("eg", [P, 2, C])
        hT = sb("hT", [P, NHC, C])
        in_range = sb("in_range", [P, CT * 4, GROUPS])
        v_peak = sb("v_peak", [P, NCH, GROUPS])
        v_small = sb("v_small", [P, NCH * GROUPS])
        fast_ok = sb("fast_ok", [P, 4])
        flag = sb("flag", [1, 1], I32)

        x_loaded = [sem(f"x_loaded{c}") for c in range(NCH)]
        w_qkv_loaded = sem("w_qkv_loaded")
        w_o_loaded = sem("w_o_loaded")
        w_ffn_loaded = sem("w_ffn_loaded")
        rope_loaded = sem("rope_loaded")
        ident_ready = sem("ident_ready")
        vs_preset = sem("vs_preset")
        ffn_dequantised = sem("ffn_dequantised")
        product_ready = sem("product_ready")
        act_emptied = sem("act_emptied")
        dve_emptied = sem("dve_emptied")
        exp_done = sem("exp_done")
        zeros_masked = sem("zeros_masked")
        causal_masked = sem("causal_masked")
        pv_done = sem("pv_done")
        o_copied = sem("o_copied")
        part_ready = sem("part_ready")
        v_checked = sem("v_checked")
        fast_ok_ready = sem("fast_ok_ready")
        mask_ready = sem("mask_ready")
        stacks_fetched = sem("stacks_fetched")
        scored = sem("scored")
        maximum_ready = sem("maximum_ready")
        exponentiated = sem("exponentiated")
        probs_ready = sem("probs_ready")
        transposed = sem("transposed")
        keys_first = sem("keys_first")
        summed = sem("summed")
        head_done = sem("head_done")
        tile_products = sem("tile_products")
        tile_copies = sem("tile_copies")
        tile_rows = sem("tile_rows")
        tile_rstd = sem("tile_rstd")
        tile_written = sem("tile_written")
        stack_written = [sem(f"stack_written{c}") for c in range(NCH)]
        stacks_loaded = [sem(f"stacks_loaded{k}") for k in range(len(blocks))]
        dve_chain = sem("dve_chain")
        pool_chain = sem("pool_chain")
        stats_ready = sem("stats_ready")
        rstd_ready = sem("rstd_ready")
        rows_normalised = sem("rows_normalised")
        hidden_ready = sem("hidden_ready")
        out_written = [sem(f"out_written{i}") for i in range(2)]

        block = ctx.enter_context(nc.Block())

        def number(items, it):
            return items.index(it) + 1

        def home(it):
            if it[0] == "score":
                return slots[scores.index(it) % RING]
            if it in side_items:
                return side
            if it[1] == tail and it[0] not in ("xT", "q", "k"):
                bank, half = {"oT": (0, it[-1]), "onT": (1, 0), "proj": (1, 1), "x1T": (2, 1), "gate": (it[-1], 0),
                              "up": (it[-1], 1), "down": (0, 0)}[it[0]]
                return slots[bank][:, half]
            return {"q": slots[0][:, 0], "k": slots[0][:, 1], "xT": slots[1][:, 0]}[it[0]]

        wide = [p_sb[:, i].rearrange("p a c -> p (a c)") for i in range(NP)]
        masked, keep, probs, probsT, low = wide[0], wide[1], wide[2], wide[3], wide[6]
        causal = p_sb[:, 4:6].rearrange("p n a c -> p (n a c)")
        v_head = wide[7][:, 0:NT * DH].rearrange("p (t d) -> p t d", d=DH)
        attn_rows, attnT = wide[7][:, P:2 * P], wide[7][:, 2 * P:3 * P]
        top, shift, den, inv = (wide[7][:, 3 * P + i:3 * P + i + 1] for i in range(4))
        row, row_T = y[:, 0, 0], y[:, 0, 1]
        row_eg, row_h = gu[:, 0, 0, 0:HID], gu[:, 0, 1, 0:HID]

        def flag_of(eng):
            eng.wait_ge(dve_emptied, number(by_dve, ("flag", None)))
            return eng.value_load(flag[0:1, 0:1], min_val=0, max_val=1)

        def careful(eng, head_work, tile_work):
            with eng.Fori(0, B) as b:
                with eng.Fori(0, HALVES) as half:
                    with eng.Fori(0, CT) as t:
                        tiles = b * NT + half * CT + t
                        with eng.Fori(0, HEADS // 2) as pair:
                            with eng.Fori(0, 2) as g:
                                head_work(b, half, t, pair, g, tiles * HEADS + pair * 2 + g)
                        if tile_work is not None:
                            tile_work(tiles)

        def last_product(k):
            return number(slotted, [i for i in scores if i[1:4] == blocks[k]][-1])

        def wait_product(eng, it):
            eng.wait_ge(product_ready, number(slotted, it))

        def wait_emptied(eng, it):
            if it[0] == "score":
                eng.wait_ge(zeros_masked, number(scores, it))
            elif it in by_act:
                eng.wait_ge(act_emptied, number(by_act, it))
            else:
                eng.wait_ge(dve_emptied, number(by_dve, it))

        chunk_rows = x.rearrange("b (c t p) d -> (b c) p t d", c=HALVES, p=P)
        out_rows = out.rearrange("b (c t p) d -> (b c) p t d", c=HALVES, p=P)

        def key_halves(k):
            b, half, st = blocks[k]
            had = {h for bb, h, ss in blocks[:k] if (bb, ss) == (b, st)}
            return [h for h in range(half + 1) if not had or h > max(had)]

        @block.sync
        def _(sp):
            sp.dma_start(w_qkv[:], qkv.rearrange("(t p) d -> p t d", p=P)).then_inc(w_qkv_loaded, 16)
            sp.dma_start(cos_sb[:], cos_t).then_inc(rope_loaded, 16)
            sp.dma_start(sin_sb[:], sin_t).then_inc(rope_loaded, 16)
            sp.dma_start(x_sb[:, CT:2 * CT, :], chunk_rows[1]).then_inc(x_loaded[1], 16)
            sp.dma_start(w_o[:], wo).then_inc(w_o_loaded, 16)
            for c in range(2, NCH):
                sp.dma_start(x_sb[:, c * CT:(c + 1) * CT, :], chunk_rows[c]).then_inc(x_loaded[c], 16)
            for n, w in enumerate((w_gate, w_up)):
                sp.dma_start(w_ffn_i[:, n, :].rearrange("p (t d) -> p t d", t=NHC),
                             w.rearrange("(t p) d -> p t d", p=P)).then_inc(w_ffn_loaded, 16)
            sp.dma_start(w_ffn_i[:, 2, :], w_down).then_inc(w_ffn_loaded, 16)
            for it in plan:
                if it[0] in ("q", "k") and it[1] == 0 or it[0] == "rotate" and it[3] == 7:
                    c = it[1]
                    n = it[2] if it[0] == "rotate" else "qk".index(it[0])
                    for part in range(3):
                        sp.wait_ge(part_ready, 3 * (2 * c + n) + part + 1)
                        sp.dma_start(stacks[c, n, part], parts[:, n, part]).then_inc(stack_written[c], 16)
                if it[0] == "load":
                    k = it[1]
                    b, half, st = blocks[k]
                    if k >= 2:
                        sp.wait_ge(product_ready, last_product(k - 2))
                    mine = slice(st * SH * C, (st + 1) * SH * C)
                    for h in key_halves(k):
                        c = b * HALVES + h
                        sp.wait_ge(stack_written[c], 6 * 16)
                        src = stacks[c, 1].rearrange("t (d h) s -> (t d) (h s)", d=DH)[:, mine]
                        sp.dma_start(ks[:, st, h].rearrange("p h s -> p (h s)"),
                                     src.unsqueeze(0).to_broadcast([3, 3 * DH, SH * C])).then_inc(stacks_loaded[k], 16)
                    c = b * HALVES + half
                    for part in range(3):
                        src = stacks[c, 0, part].rearrange("(d h) s -> d (h s)", d=DH)[:, mine]
                        sp.dma_start(qs[3 * DH * part:3 * DH * (part + 1), k % 2].rearrange("p h s -> p (h s)"),
                                     src.unsqueeze(0).to_broadcast([3, DH, SH * C])).then_inc(stacks_loaded[k], 16)
                if it[0] == "scale" and it[2] == 1:
                    e = finishing.index(it[1])
                    sp.wait_ge(rows_normalised, 2 * e + 2)
                    sp.dma_start(out_rows[it[1]], y[:, e % 2]).then_inc(out_written[e % 2], 16)
            ok = flag_of(sp)
            for i in range(2):
                sp.wait_ge(out_written[i], 16 * NCH // 2)

            def fetch(b, half, t, pair, g, n):
                sp.wait_ge(head_done, n + 1)
                rows_of = lambda c, i: stacks[c, i].rearrange("t (d h) s -> t d h s", d=DH)
                for h in range(HALVES):
                    src = stacks[bass.ds(b * HALVES + h, 1), 1].rearrange("o t (d h) s -> h (o t d) s", d=DH)
                    src = src[bass.ds(pair * 2 + g, 1)].to_broadcast([3, 3 * DH, C])
                    sp.dma_start(ks[:, 0, 0, h], src).then_inc(stacks_fetched, 16)
                for part in range(3):
                    src = stacks[bass.ds(b * HALVES + half, 1), 0, part].rearrange("o (d h) s -> h (o d) s", d=DH)
                    src = src[bass.ds(pair * 2 + g, 1), :, bass.ds(t * P, P)].to_broadcast([3, DH, P])
                    sp.dma_start(qs[3 * DH * part:3 * DH * (part + 1), 0, 0, 0:P], src).then_inc(stacks_fetched, 16)

            def send(tiles):
                sp.wait_ge(tile_rows, 5 * tiles + 5)
                sp.dma_start(out.rearrange("b s d -> (b s) d")[bass.ds(tiles * P, P)], row).then_inc(tile_written, 16)

            with sp.If(ok == 0):
                careful(sp, fetch, send)
                sp.wait_ge(tile_written, 16 + 16 * B * NT)

        def rotate_step(eng, nce, link, c, n, src, step):
            cs = slice(c % HALVES * C, (c % HALVES + 1) * C)
            if step == 0:
                if n == 1 or c:
                    eng.wait_ge(part_ready, 3 * (2 * c + n))
                link(nce.tensor_tensor(rot[:, 0], src[:], cos_sb[:, cs], ALU.mult))
            elif step in (1, 2):
                lo, hi = ((0, 64), (64, 0))[step - 1]
                link(nce.tensor_tensor(rot[lo:lo + 64, 1], src[hi:hi + 64], sin_sb[hi:hi + 64, cs], ALU.mult))
            elif step == 3:
                link(nce.tensor_tensor(qk[:, n], rot[:, 0], rot[:, 1], ALU.add))
            elif step == 4:
                if c > 0:
                    eng.wait_ge(stack_written[c - 1], 6 * 16)
                nce.tensor_copy(parts[:, n, 0], qk[:, n]).then_inc(part_ready, 1)
            elif step == 5:
                eng.wait_ge(part_ready, 3 * (2 * c + n) + 1)
                link(nce.tensor_tensor(rot[:, 0], qk[:, n], parts[:, n, 0], ALU.subtract))
            elif step == 6:
                nce.tensor_copy(parts[:, n, 1], rot[:, 0]).then_inc(part_ready, 1)
            else:
                eng.wait_ge(part_ready, 3 * (2 * c + n) + 2)
                nce.tensor_tensor(parts[:, n, 2], rot[:, 0], parts[:, n, 1], ALU.subtract).then_inc(part_ready, 1)

        @block.gpsimd
        def _(pool):
            chain = [0]

            def link(ins):
                chain[0] += 1
                ins.then_inc(pool_chain, 1)
                pool.wait_ge(pool_chain, chain[0])

            link(nc.gpsimd.memset(ident[:], 0.0))
            nc.gpsimd.affine_select(out=ident[:], in_=ident[:], compare_op=ALU.not_equal, fill=1.0, base=0,
                                    pattern=[[-1, P]], channel_multiplier=1).then_inc(ident_ready, 1)
            link(nc.gpsimd.memset(vs[:, 0:CT], 0.0))
            for g in range(GROUPS):
                last = nc.gpsimd.memset(vs[:, 0:CT, :, g, 16 + 8 * g:24 + 8 * g], 1.0)
            last.then_inc(vs_preset, 1)
            link(nc.gpsimd.memset(vs[:, CT:B * NT], 0.0))
            for g in range(GROUPS):
                last = nc.gpsimd.memset(vs[:, CT:B * NT, :, g, 16 + 8 * g:24 + 8 * g], 1.0)
            last.then_inc(vs_preset, 1)
            link(nc.gpsimd.memset(minus_half[:], -0.5))
            pool.wait_ge(w_ffn_loaded, 48)
            nc.gpsimd.tensor_scalar(w_ffn, w_ffn_i[:], DEQUANT, None, ALU.mult).then_inc(ffn_dequantised, 1)

            done = {"masks": 0, "rstd": 0, "hidden": 0}
            for it in plan:
                kind = it[0]
                if kind == "rotate":
                    _, c, n, step = it
                    if step == 0:
                        pool.wait_ge(act_emptied, number(by_act, ("qk"[n], c)))
                    if step in (1, 2):
                        pool.wait_ge(causal_masked, done["masks"])
                        if done["rstd"]:
                            pool.wait_ge(rstd_ready, done["rstd"])
                        if done["hidden"]:
                            pool.wait_ge(hidden_ready, done["hidden"])
                    rotate_step(pool, nc.gpsimd, link, c, n, raw[:, n], step)
                elif kind == "score" and it in diagonal:
                    u = scores.index(it)
                    blk = p_sb[:, u % NP].rearrange("p a c -> p (a c)")
                    diag = units[it[2]][it[5]][1]
                    views = {"first": [blk.rearrange("p (a c) -> p a c", a=2)[:, :, 0:P]],
                             "outer": [blk.rearrange("p (a c) -> p a c", a=2)[:, :, lo:lo + P] for lo in (0, 3 * P)],
                             "inner": [blk.rearrange("p (a c) -> p a c", a=4)[:, :, 0:P]]}[diag]
                    pool.wait_ge(zeros_masked, u + 1)
                    for view in views:
                        last = nc.gpsimd.affine_select(out=view, in_=view, compare_op=ALU.is_ge, fill=0.0, base=0,
                                                       pattern=[[0, view.shape[1]], [1, P]], channel_multiplier=-1)
                    last.then_inc(causal_masked, 1)
                    done["masks"] += 1
                elif kind == "stats":
                    n = 2 * finishing.index(it[1]) + it[2]
                    pool.wait_ge(stats_ready, n + 1)
                    nc.gpsimd.tensor_tensor(rstd[:], ve[:], minus_half[:], ALU.pow).then_inc(rstd_ready, 1)
                    done["rstd"] += 1
                elif kind == "gate" and it[1] != tail:
                    m = (3 * finishing.index(it[1]) + it[2]) % 2
                    pool.wait_ge(act_emptied, number(by_act, it))
                    link(nc.gpsimd.tensor_scalar(eg[:, m], eg[:, m], 1.0, 0.5, ALU.add, ALU.mult))
                    link(nc.gpsimd.tensor_tensor(eg[:, m], gu[:, m, 0], eg[:, m], ALU.mult))
                elif kind == "up" and it[1] != tail:
                    e, hc = finishing.index(it[1]), it[2]
                    m = (3 * e + hc) % 2
                    pool.wait_ge(act_emptied, number(by_act, it))
                    if e:
                        pool.wait_ge(product_ready, number(slotted, ("down", finishing[e - 1])))
                    nc.gpsimd.tensor_tensor(hT[:, hc], gu[:, m, 1], eg[:, m], ALU.mult).then_inc(hidden_ready, 1)
                    done["hidden"] += 1

            with pool.If(flag_of(pool) == 0):
                pool.wait_ge(rows_normalised, 2 * NCH)
                nc.gpsimd.memset(causal[:], 1.0).then_inc(mask_ready, 1)
                pool.wait_ge(mask_ready, 1)
                nc.gpsimd.affine_select(out=causal[:], in_=causal[:], compare_op=ALU.is_ge, fill=0.0,
                                        base=(NT - 1) * P, pattern=[[-1, 2 * S]],
                                        channel_multiplier=1).then_inc(mask_ready, 1)
                with pool.Fori(0, B * NT) as tiles:
                    for half in range(2):
                        pool.wait_ge(tile_rows, 5 * tiles + (1, 4)[half])
                        nc.gpsimd.tensor_tensor(rstd[:, 0:1], ve[:, 0:1], minus_half[:, 0:1],
                                                ALU.pow).then_inc(tile_rstd, 1)

        @block.scalar
        def _(act):
            act.dma_start(x_sb[:, 0:CT, :], chunk_rows[0]).then_inc(x_loaded[0], 16)
            for it in plan:
                kind = it[0]
                if it in by_act:
                    wait_product(act, it)
                if kind == "xT":
                    if it[1] >= 2:
                        wait_product(act, ("v", it[1] - 2))
                    nc.scalar.activation(xT[:, it[1] % 2], home(it)[:], ACT.Copy).then_inc(act_emptied, 1)
                elif kind in ("q", "k") and it[1] > 0:
                    if it[1] > 1:
                        act.wait_ge(part_ready, 3 * (number(qk_items, it) - 2))
                    nc.scalar.activation(raw[:, "qk".index(kind)], side[:], ACT.Copy).then_inc(act_emptied, 1)
                elif kind == "v":
                    c = it[1]
                    act.wait_ge(vs_preset, 1 if c == 0 else 2)
                    src = side[:].rearrange("p (t j g d) -> p t j g d", t=CT, g=GROUPS, d=DH)
                    for g in range(GROUPS):
                        last = nc.scalar.activation(vs[:, c * CT:(c + 1) * CT, :, g, 8 * g:8 * g + 8],
                                                    src[:, :, :, g, :], ACT.Copy)
                    last.then_inc(act_emptied, 1)
                elif kind == "ffnw":
                    nc.scalar.activation(ffT[:, it[1]], side[:, 0:HID], ACT.Copy).then_inc(act_emptied, 1)
                elif kind == "score":
                    u = scores.index(it)
                    wait_product(act, it)
                    if u >= NP:
                        act.wait_ge(pv_done, u - NP + 1)
                    nc.scalar.activation(p_sb[:, u % NP].rearrange("p a c -> p (a c)"),
                                         home(it)[:].rearrange("p a c -> p (a c)"), ACT.Exp,
                                         scale=SCORE_SCALE).then_inc(exp_done, 1)
                elif kind == "outputs":
                    k = it[1]
                    last_unit = max(u for u, i in enumerate(scores) if i[1:4] == blocks[k])
                    act.wait_ge(pv_done, last_unit + 1)
                    if k >= 2:
                        wait_product(act, ("oT", finishing[k // 2 - 1], k % 2))
                    nc.scalar.activation(o_sb[:, k % 2], o_acc[:], ACT.Copy).then_inc(o_copied, 1)
                elif kind == "onT":
                    e = finishing.index(it[1])
                    if e:
                        wait_product(act, ("proj", finishing[e - 1]))
                    nc.scalar.activation(o_n[:], home(it)[:], ACT.Copy).then_inc(act_emptied, 1)
                elif kind == "x1T":
                    e = finishing.index(it[1])
                    if e:
                        wait_product(act, ("up", finishing[e - 1], 2))
                    nc.scalar.activation(x1T[:], home(it)[:], ACT.Copy).then_inc(act_emptied, 1)
                elif kind == "gate":
                    n = 3 * finishing.index(it[1]) + it[2]
                    if n >= 2:
                        act.wait_ge(hidden_ready, n - 1)
                    last = nc.scalar.activation(eg[:, n % 2], home(it)[:], ACT.Tanh, scale=0.5)
                    if it[1] != tail:
                        last = nc.scalar.activation(gu[:, n % 2, 0], side[:], ACT.Copy)
                    last.then_inc(act_emptied, 1)
                elif kind == "up" and it[1] != tail:
                    n = 3 * finishing.index(it[1]) + it[2]
                    nc.scalar.activation(gu[:, n % 2, 1], side[:], ACT.Copy).then_inc(act_emptied, 1)

            def head(b, half, t, pair, g, n):
                act.wait_ge(maximum_ready, n + 1)
                nc.scalar.activation(probs, masked, ACT.Exp, bias=shift, scale=SCORE_SCALE).then_inc(exponentiated, 1)
                act.wait_ge(transposed, n + 1)
                nc.scalar.activation(probsT, slots[1][:].rearrange("p a c -> p (a c)"),
                                     ACT.Copy).then_inc(keys_first, 1)

            def tile(tiles):
                act.wait_ge(tile_products, 5 * tiles + 1)
                nc.scalar.activation(attnT, side[:, 0:P], ACT.Copy).then_inc(tile_copies, 1)
                act.wait_ge(tile_products, 5 * tiles + 3)
                nc.scalar.activation(row_T, side[:, 0:P], ACT.Copy).then_inc(tile_copies, 1)
                act.wait_ge(tile_products, 5 * tiles + 4)
                nc.scalar.activation(row_eg, slots[0][:, 0, 0:HID], ACT.Tanh, scale=0.5).then_inc(tile_copies, 1)

            with act.If(flag_of(act) == 0):
                careful(act, head, tile)

        @block.vector
        def _(dve):
            chain = [0]

            def link(ins):
                chain[0] += 1
                ins.then_inc(dve_chain, 1)
                dve.wait_ge(dve_chain, chain[0])

            link(nc.vector.memset(in_range[:], 1.0))
            for it in plan:
                kind = it[0]
                if kind == "weights":
                    wait_product(dve, it)
                    for n in range(2):
                        nc.vector.tensor_copy(wT[:, n].rearrange("p (d h) -> p d h", d=DH),
                                              side[:, n * P:(n + 1) * P].rearrange("p (h d) -> p d h", d=DH))
                    nc.vector.tensor_copy(wT[:, 2], side[:, 2 * P:3 * P])
                    nc.vector.tensor_copy(woT[:], side[:, 3 * P:4 * P]).then_inc(dve_emptied, 1)
                elif kind in ("q", "k") and it[1] == 0:
                    wait_product(dve, it)
                    dve.wait_ge(rope_loaded, 32)
                    for step in range(8):
                        rotate_step(dve, nc.vector, link, 0, "qk".index(kind), home(it), step)
                elif kind == "v":
                    c = it[1]
                    dve.wait_ge(act_emptied, number(by_act, it))
                    for g in range(GROUPS):
                        last = nc.vector.tensor_reduce(v_peak[:, c, g:g + 1],
                                                       vs[:, c * CT:(c + 1) * CT, :, g, 8 * g:8 * g + 8],
                                                       AX_XYZ, ALU.max, apply_absolute_value=True)
                    last.then_inc(v_checked, 1)
                elif kind == "score":
                    u = scores.index(it)
                    dve.wait_ge(exp_done, u + 1)
                    e = p_sb[:, u % NP].rearrange("p a c -> p (a c)")
                    nc.vector.scalar_tensor_tensor(out=e, in0=home(it)[:].rearrange("p a c -> p (a c)"),
                                                   scalar=0.0, in1=e, op0=ALU.not_equal,
                                                   op1=ALU.mult).then_inc(zeros_masked, 1)
                elif kind == "oT":
                    e, st = finishing.index(it[1]), it[2]
                    wait_product(dve, it)
                    strips = home(it)[:].rearrange("p (t r) -> p t r", r=32)
                    link(nc.vector.reciprocal(den_inv[:, st], strips[:, :, 16:32:8]))
                    link(nc.vector.scalar_tensor_tensor(out=in_range[:], in0=den_inv[:, st], scalar=1.0 / WINDOW,
                                                        in1=in_range[:], op0=ALU.is_ge, op1=ALU.mult))
                    link(nc.vector.scalar_tensor_tensor(out=in_range[:], in0=den_inv[:, st], scalar=WINDOW,
                                                        in1=in_range[:], op0=ALU.is_le, op1=ALU.mult))
                    if e:
                        wait_product(dve, ("onT", finishing[e - 1]))
                    for g in range(GROUPS):
                        last = nc.vector.tensor_tensor(
                            o_rows[:, :, st].rearrange("p t (j g d) -> p t j g d", g=GROUPS, d=DH)[:, :, :, g],
                            strips[:, :, 8 * g:8 * g + 8].rearrange("p (t j) d -> p t j d", j=4),
                            den_inv[:, st, :, g:g + 1].rearrange("p (t j) o -> p t j o", j=4)
                            .to_broadcast([P, CT, 4, DH]), ALU.mult)
                    last.then_inc(dve_emptied, 1)
                elif kind == "flag":
                    dve.wait_ge(v_checked, NCH)
                    link(nc.vector.tensor_reduce(fast_ok[:, 0:1], in_range[:].rearrange("p a g -> p (a g)"), AX_X, ALU.min))
                    link(nc.vector.tensor_scalar(v_small[:], v_peak[:].rearrange("p c g -> p (c g)"), V_LIMIT, None,
                                                 ALU.is_le))
                    link(nc.vector.tensor_reduce(fast_ok[:, 1:2], v_small[:], AX_X, ALU.min))
                    nc.vector.tensor_tensor(fast_ok[:, 2:3], fast_ok[:, 0:1], fast_ok[:, 1:2],
                                            ALU.mult).then_inc(fast_ok_ready, 1)
                    wait_product(dve, it)
                    link(nc.vector.tensor_reduce(fast_ok[0:1, 3:4], side[0:1, 0:P], AX_X, ALU.min))
                    nc.vector.tensor_copy(flag[:], fast_ok[0:1, 3:4]).then_inc(dve_emptied, 1)
                elif kind in ("proj", "down"):
                    e = finishing.index(it[1])
                    wait_product(dve, it)
                    rows = y[:, e % 2].rearrange("p t d -> p (t d)")
                    if kind == "proj":
                        dve.wait_ge(x_loaded[it[1]], 16)
                        if e >= 2:
                            dve.wait_ge(out_written[e % 2], 16 * (e // 2))
                    other = x_sb[:, it[1] * CT:(it[1] + 1) * CT, :].rearrange("p t d -> p (t d)")
                    nc.vector.tensor_tensor(rows, home(it)[:], other if kind == "proj" else rows,
                                            ALU.add).then_inc(dve_emptied, 1)
                elif kind == "stats":
                    e, which = finishing.index(it[1]), it[2]
                    dve.wait_ge(dve_emptied, number(by_dve, (("proj", "down")[which], it[1])))
                    if 2 * e + which:
                        dve.wait_ge(rows_normalised, 2 * e + which)
                    for t in range(CT):
                        last = nc.vector.bn_stats(st6[:, t], y[:, e % 2, t])
                    link(last)
                    for t in range(CT):
                        last = nc.vector.bn_aggr(mv[:, t], st6[:, t])
                    link(last)
                    nc.vector.tensor_scalar(ve[:], mv[:, :, 1], EPS, None, ALU.add).then_inc(stats_ready, 1)
                elif kind == "scale":
                    e, which = finishing.index(it[1]), it[2]
                    dve.wait_ge(rstd_ready, 2 * e + which + 1)
                    for t in range(CT):
                        last = nc.vector.tensor_scalar(y[:, e % 2, t], y[:, e % 2, t], mv[:, t, 0:1], rstd[:, t:t + 1],
                                                       ALU.subtract, ALU.mult)
                    last.then_inc(rows_normalised, 1)
                elif kind == "up" and it[1] == tail:
                    n = 3 * finishing.index(it[1]) + it[2]
                    dve.wait_ge(act_emptied, number(by_act, ("gate", *it[1:])))
                    link(nc.vector.tensor_scalar(eg[:, n % 2], eg[:, n % 2], 1.0, 0.5, ALU.add, ALU.mult))
                    link(nc.vector.tensor_tensor(eg[:, n % 2], home(("gate", *it[1:]))[:], eg[:, n % 2], ALU.mult))
                    wait_product(dve, it)
                    nc.vector.tensor_tensor(hT[:, it[2]], home(it)[:], eg[:, n % 2], ALU.mult).then_inc(hidden_ready, 1)

            def head(b, half, t, pair, g, n):
                dve.wait_ge(scored, n + 1)
                s = slots[0][:].rearrange("p a c -> p (a c)")
                done = (NT - 1) * P - half * C - t * P
                nc.vector.scalar_tensor_tensor(out=keep, in0=s, scalar=0.0, in1=causal[:, bass.ds(done, S)],
                                               op0=ALU.not_equal, op1=ALU.mult)
                dve.drain()
                nc.vector.tensor_tensor(masked, s, keep, ALU.mult)
                nc.vector.tensor_scalar(low, keep, 1.0, 3e38, ALU.subtract, ALU.mult)
                dve.drain()
                nc.vector.tensor_tensor(masked, masked, low, ALU.add)
                dve.drain()
                nc.vector.tensor_reduce(top, masked, AX_X, ALU.max)
                dve.drain()
                nc.vector.tensor_scalar(shift, top, -SCORE_SCALE, None, ALU.mult).then_inc(maximum_ready, 1)
                nc.vector.tensor_copy(v_head, vs[:].rearrange("p t j g r -> p t j (g r)")
                                      [:, bass.ds(b * NT, NT), bass.ds(pair, 1), bass.ds(g * (32 + DH), DH)]
                                      .rearrange("p t o d -> p t (o d)"))
                dve.wait_ge(exponentiated, n + 1)
                nc.vector.tensor_tensor(probs, probs, keep, ALU.mult)
                dve.drain()
                nc.vector.tensor_reduce(den, probs, AX_X, ALU.add)
                dve.drain()
                nc.vector.reciprocal(inv, den).then_inc(probs_ready, 1)
                dve.wait_ge(summed, n + 1)
                nc.vector.tensor_scalar(attn_rows[:, bass.ds(pair * (2 * DH) + g * DH, DH)], o_acc[:, 0:DH], inv, None,
                                        ALU.mult).then_inc(head_done, 1)

            def norm_stats():
                dve.drain()
                nc.vector.bn_stats(st6[:, 0], row)
                dve.drain()
                nc.vector.bn_aggr(mv[:, 0], st6[:, 0])
                dve.drain()
                nc.vector.tensor_scalar(ve[:, 0:1], mv[:, 0, 1:2], EPS, None, ALU.add).then_inc(tile_rows, 1)

            def norm_scale():
                nc.vector.tensor_scalar(row, row, mv[:, 0, 0:1], rstd[:, 0:1], ALU.subtract,
                                        ALU.mult).then_inc(tile_rows, 1)

            def tile(tiles):
                dve.wait_ge(tile_written, 16 * tiles + 16)
                dve.wait_ge(tile_products, 5 * tiles + 2)
                nc.vector.tensor_tensor(row, side[:, P:2 * P],
                                        x_sb[:, bass.ds(tiles, 1)].rearrange("p o d -> p (o d)"), ALU.add)
                norm_stats()
                dve.wait_ge(tile_rstd, 2 * tiles + 1)
                norm_scale()
                dve.wait_ge(tile_copies, 3 * tiles + 3)
                nc.vector.tensor_scalar(row_eg, row_eg, 1.0, 0.5, ALU.add, ALU.mult)
                dve.drain()
                nc.vector.tensor_tensor(row_eg, slots[0][:, 0, 0:HID], row_eg, ALU.mult)
                dve.drain()
                nc.vector.tensor_tensor(row_h, slots[1][:, 0, 0:HID], row_eg, ALU.mult).then_inc(tile_rows, 1)
                dve.wait_ge(tile_products, 5 * tiles + 5)
                nc.vector.tensor_tensor(row, side[:, 0:P], row, ALU.add)
                norm_stats()
                dve.wait_ge(tile_rstd, 2 * tiles + 2)
                norm_scale()

            with dve.If(flag_of(dve) == 0):
                dve.wait_ge(mask_ready, 2)
                nc.vector.memset(attnT, 0.0).then_inc(tile_written, 16)
                nc.vector.memset(attn_rows, 0.0).then_inc(head_done, 1)
                careful(dve, head, tile)

        @block.tensor
        def _(pe):
            def mm(o, lhsT, rhs, start=True, stop=True, **kw):
                return nc.tensor.matmul(o, lhsT, rhs, start=start, stop=stop, **kw)

            for it in plan:
                kind = it[0]
                if it in side_items[1:]:
                    wait_emptied(pe, side_items[side_items.index(it) - 1])
                if kind == "weights":
                    pe.wait_ge(ident_ready, 1)
                    pe.wait_ge(w_qkv_loaded, 16)
                    for n in range(3):
                        nc.tensor.transpose(side[:, n * P:(n + 1) * P], w_qkv[:, n], ident[:])
                    pe.wait_ge(w_o_loaded, 16)
                    last = nc.tensor.transpose(side[:, 3 * P:4 * P], w_o[:], ident[:])
                elif kind == "xT":
                    c = it[1]
                    pe.wait_ge(x_loaded[c], 16)
                    for t in range(CT):
                        last = nc.tensor.transpose(home(it)[:, t * P:(t + 1) * P], x_sb[:, c * CT + t], ident[:])
                elif kind in ("q", "k"):
                    c, n = it[1], "qk".index(kind)
                    wait_emptied(pe, ("weights",))
                    pe.wait_ge(act_emptied, number(by_act, ("xT", c)))
                    last = mm(home(it)[:], wT[:, n], xT[:, c % 2])
                elif kind == "v":
                    c = it[1]
                    for t in range(CT):
                        last = mm(side[:, t * P:(t + 1) * P], xT[:, c % 2, t * P:(t + 1) * P], wT[:, 2])
                elif kind == "ffnw":
                    pe.wait_ge(ffn_dequantised, 1)
                    for hc in range(NHC):
                        last = nc.tensor.transpose(side[:, hc * P:(hc + 1) * P],
                                                   w_ffn[:, it[1], hc * P:(hc + 1) * P], ident[:])
                elif kind == "score":
                    _, b, half, st, g, n, _ = it
                    k, u = blocks.index((b, half, st)), scores.index(it)
                    if u >= RING:
                        pe.wait_ge(zeros_masked, u - RING + 1)
                    pe.wait_ge(stacks_loaded[k], 16 * (3 + len(key_halves(k))))
                    for jp, jl, i, col, width, first in units[half][n][0]:
                        head = 4 * jp + 2 * jl + g
                        last = mm(home(it)[:, jl, col:col + width],
                                  ks[:, st, i // CT, head, (i % CT) * P:(i % CT + 1) * P],
                                  qs[:, k % 2, head, first:first + width])
                elif kind == "pv":
                    u = it[1]
                    _, b, half, st, g, n, block_ends = scores[u]
                    k = blocks.index((b, half, st))
                    pieces, diag, done = units[half][n]
                    if not done:
                        continue
                    if diag:
                        pe.wait_ge(causal_masked, number(diagonal, scores[u]))
                    else:
                        pe.wait_ge(zeros_masked, u + 1)
                    if g == 0 and done[0] == 0:
                        pe.wait_ge(act_emptied, number(by_act, ("v", b * HALVES + half)))
                        if k:
                            pe.wait_ge(o_copied, k)
                    held = [(u + m, piece) for m in range(-1 if diag != "inner" else 0, 1)
                            for piece in units[half][n + m][0]]
                    for tile in done:
                        for v, (jp, jl, i, col, width, first) in held:
                            if i != tile:
                                continue
                            j = 2 * jp + jl
                            last = mm(o_acc[32 * j:32 * j + 32, first:first + width],
                                      vs[:, b * NT + i, 4 * st + j, g, :],
                                      p_sb[:, v % NP, jl, col:col + width],
                                      start=(g == 0 and i == 0), stop=(block_ends and jp == 1 and jl == 1),
                                      skip_group_check=True)
                    last.then_inc(pv_done, 1 if diag == "inner" else 2)
                elif kind == "oT":
                    e, st = finishing.index(it[1]), it[2]
                    pe.wait_ge(o_copied, 2 * e + st + 1)
                    for t in range(CT):
                        last = nc.tensor.transpose(home(it)[:, t * P:(t + 1) * P], o_sb[:, st, t * P:(t + 1) * P],
                                                   ident[:])
                elif kind == "onT":
                    wait_emptied(pe, ("oT", it[1], 1))
                    for t in range(CT):
                        last = nc.tensor.transpose(home(it)[:, t * P:(t + 1) * P],
                                                   o_rows[:, t].rearrange("p a r -> p (a r)"), ident[:])
                elif kind == "proj":
                    wait_emptied(pe, ("onT", it[1]))
                    for t in range(CT):
                        last = mm(home(it)[:, t * P:(t + 1) * P], o_n[:, t * P:(t + 1) * P], woT[:])
                elif kind == "x1T":
                    e = finishing.index(it[1])
                    pe.wait_ge(rows_normalised, 2 * e + 1)
                    for t in range(CT):
                        last = nc.tensor.transpose(home(it)[:, t * P:(t + 1) * P], y[:, e % 2, t], ident[:])
                elif kind == "flag":
                    pe.wait_ge(fast_ok_ready, 1)
                    last = mm(side[0:1, 0:P], fast_ok[:, 2:3], ident[:])
                elif kind in ("gate", "up"):
                    wait_emptied(pe, ("x1T", it[1]))
                    last = mm(home(it)[:], ffT[:, ("gate", "up").index(kind), it[2] * P:(it[2] + 1) * P], x1T[:])
                elif kind == "down":
                    e = finishing.index(it[1])
                    pe.wait_ge(hidden_ready, 3 * e + 3)
                    for t in range(CT):
                        for hc in range(NHC):
                            last = mm(home(it)[:, t * P:(t + 1) * P], hT[:, hc, t * P:(t + 1) * P],
                                      ffT[:, 2, hc * P:(hc + 1) * P], start=(hc == 0), stop=(hc == NHC - 1))
                if it in slotted:
                    last.then_inc(product_ready, 1)

            def head(b, half, t, pair, g, n):
                pe.wait_ge(stacks_fetched, 80 * n + 80)
                for h in range(HALVES):
                    last = mm(slots[0][:, h], qs[:, 0, 0, 0:P], ks[:, 0, 0, h])
                last.then_inc(scored, 1)
                pe.wait_ge(probs_ready, n + 1)
                for i in range(NT):
                    last = nc.tensor.transpose(slots[1][:, i // CT, (i % CT) * P:(i % CT + 1) * P],
                                               probs[:, i * P:(i + 1) * P], ident[:])
                last.then_inc(transposed, 1)
                pe.wait_ge(keys_first, n + 1)
                for i in range(NT):
                    last = mm(o_acc[:, 0:DH], probsT[:, i * P:(i + 1) * P], v_head[:, i], start=i == 0, stop=i == NT - 1)
                last.then_inc(summed, 1)

            def tile(tiles):
                pe.wait_ge(head_done, HEADS * tiles + HEADS + 1)
                nc.tensor.transpose(side[:, 0:P], attn_rows, ident[:]).then_inc(tile_products, 1)
                pe.wait_ge(tile_copies, 3 * tiles + 1)
                mm(side[:, P:2 * P], attnT, woT[:]).then_inc(tile_products, 1)
                pe.wait_ge(tile_rows, 5 * tiles + 2)
                nc.tensor.transpose(side[:, 0:P], row, ident[:]).then_inc(tile_products, 1)
                pe.wait_ge(tile_copies, 3 * tiles + 2)
                for n in range(2):
                    for hc in range(NHC):
                        cs = slice(hc * P, (hc + 1) * P)
                        last = mm(slots[n][:, 0, cs], ffT[:, n, cs], row_T)
                last.then_inc(tile_products, 1)
                pe.wait_ge(tile_rows, 5 * tiles + 3)
                for hc in range(NHC):
                    cs = slice(hc * P, (hc + 1) * P)
                    last = mm(side[:, 0:P], row_h[:, cs], ffT[:, 2, cs], start=hc == 0, stop=hc == NHC - 1)
                last.then_inc(tile_products, 1)

            with pe.If(flag_of(pe) == 0):
                careful(pe, head, tile)


_INS = ["L0_attn_x", "L0_attn_qkv", "L0_attn_wo", "L0_ffn_w_gate", "L0_ffn_w_up", "L0_ffn_w_down"]


def rope_tables():
    import numpy as np

    inv = (1.0 / np.float32(10000.0) ** (np.arange(0, DH, 2, dtype=np.float32) / np.float32(DH))).astype(np.float32)
    ang = np.arange(S, dtype=np.float32)[:, None] * inv[None, :]
    d = np.arange(P) // HEADS
    cos = np.cos(ang).astype(np.float32).T[d % (DH // 2)]
    sin = np.sin(ang).astype(np.float32).T[d % (DH // 2)]
    sin = np.where((d < DH // 2)[:, None], sin, -sin).astype(np.float32)
    return np.ascontiguousarray(cos), np.ascontiguousarray(sin)


def kernel(**inputs):
    import numpy as _np
    import concourse.bacc as _bacc
    from concourse import mybir as _mybir
    from concourse.bass_utils import run_bass_kernel_spmd as _run

    nc = _bacc.Bacc("TRN2", target_bir_lowering=False, num_devices=1)
    arrays, args = {}, []
    cos, sin = rope_tables()
    for name, a in [(n, inputs[n]) for n in _INS] + [("cos", cos), ("sin", sin)]:
        a = _np.ascontiguousarray(a)
        arrays[f"in_{name}_dram"] = a
        args.append(nc.dram_tensor(f"in_{name}_dram", a.shape, _mybir.dt.from_np(a.dtype), kind="ExternalInput").ap())
    args.append(nc.dram_tensor("out_0_dram", (B, S, D), F32, kind="ExternalOutput").ap())
    args.append(nc.dram_tensor("stacks_dram", (NCH, 2, 3, P, C), BF16, kind="Internal").ap())
    build(nc, *args)
    r = _run(nc, [arrays], core_ids=[0])
    return r.results[0]["out_0_dram"]
```

```python
from contextlib import ExitStack

import concourse.bass as bass
from concourse import mybir

F32 = mybir.dt.float32
BF16 = mybir.dt.bfloat16
I32 = mybir.dt.int32
ALU = mybir.AluOpType
ACT = mybir.ActivationFunctionType
AX_X, AX_XYZ = mybir.AxisListType.X, mybir.AxisListType.XYZ

P = 128
B, S, D = 2, 1024, 128
HEADS, DH = 16, 8
HID = 384
NHC = HID // P
C = 512
CT = C // P
HALVES = S // C
NCH = B * HALVES
NT = S // P
SCORE_SCALE = float(DH) ** -0.5
DEQUANT = 1.0 / 127.0
EPS = 1e-5
WINDOW, V_LIMIT = 1e20, 1e12
RING = 7
NP = 16
LAG = 7
ROTATED_BY_DVE = {(0, 0), (0, 1), (1, 0)}
SETS, GROUPS = 2, 2
SH = HEADS // SETS
TERMS = 9
ROWS = TERMS * DH


PREPARE_AT = [(13, 2.4), (50, 0.6)]
FFN_WEIGHTS_AT = [23, 24, 26]
FINISH_AT = [[27, 28, 32, 34, 35.0, 37.0, 41.0, 42.0, 42.0, 45, 46, 46, 46, 50.5, 50.5, 55],
             [6.5, 10.5, 13.5, 16.0, 17, 18, 21, 24.0, 26, 27, 28, 28, 28, 32, 32, 34.0],
             [27.5, 30.5, 32.0, 36.5, 40.0, 42, 45.5, 47, 47, 50.5, 53, 57, 60, 67.5, 67.5, 70.5],
             [50.0]]


def group_units(half):
    units = []
    first = half * CT
    for i in range(first):
        for jp in range(2):
            units.append(([(jp, jl, i, 0, C, 0) for jl in range(2)], None, [i] if jp else []))
    for jp in range(2):
        units.append(([(jp, jl, first, 0, C, 0) for jl in range(2)], "first", [first] if jp else []))
    for jp in range(2):
        pieces = []
        for jl in range(2):
            pieces += [(jp, jl, first + 1, 0, 3 * P, P), (jp, jl, first + 3, 3 * P, P, 3 * P)]
        units.append((pieces, "outer", [first + 1, first + 3] if jp else []))
    units.append(([(jp, jl, first + 2, 2 * P * jp, 2 * P, 2 * P) for jp in range(2) for jl in range(2)],
                  "inner", [first + 2]))
    halves = []
    for pieces, diag, done in units:
        for jl in range(2):
            halves.append(([p for p in pieces if p[1] == jl], diag, done if jl else []))
    return halves


def make_plan():
    def attend(b, half):
        units = group_units(half)
        return [("score", b, half, st, g, n, n == len(units) - 1 and g == 1)
                for st in range(SETS) for g in range(GROUPS) for n in range(len(units))]

    def prepare(c, at=0, step=1):
        items = [(at, ("xT", c)), (at + 1, ("q", c)), (at + 3, ("k", c)), (at + 5, ("v", c))]
        if c:
            items += [(at + 2 + step * i, ("rotate", c, i // 8, i % 8)) for i in range(16)]
        return items

    def finish(e, at):
        kinds = [("oT", e, 0), ("oT", e, 1), ("onT", e), ("proj", e), ("stats", e, 0), ("scale", e, 0), ("x1T", e),
                 ("gate", e, 0), ("up", e, 0), ("gate", e, 1), ("up", e, 1), ("gate", e, 2), ("up", e, 2),
                 ("down", e), ("stats", e, 1), ("scale", e, 1)]
        return list(zip(at, kinds))

    def weave(units, *extras):
        extra = sorted((x for xs in extras for x in xs), key=lambda x: x[0])
        out = []
        for i, u in enumerate(units):
            while extra and 2 * extra[0][0] <= i:
                out.append(extra.pop(0)[1])
            out.append(u)
        return out + [it for _, it in extra]

    plan = [("weights",)] + [("xT", 0), ("q", 0), ("load q", 0), ("k", 0), ("load k", 0), ("load q", 1), ("load k", 1),
                           ("v", 0)]
    plan += [it for _, it in prepare(1)]
    plan += weave(attend(0, 0) + attend(0, 1), prepare(2, *PREPARE_AT[0]), prepare(3, *PREPARE_AT[1]),
                  [(at, ("ffnw", n)) for n, at in enumerate(FFN_WEIGHTS_AT)], finish(0, FINISH_AT[0]))
    plan += weave(attend(1, 0) + attend(1, 1), finish(1, FINISH_AT[1]), finish(2, FINISH_AT[2]),
                  [(FINISH_AT[3][0], ("oT", 3, 0))])
    out, due, seen, block = [], [], 0, 0
    total = sum(it[0] == "score" for it in plan)
    loads = []
    order = [(0, 0), (0, 1), (1, 0), (1, 1)]

    def split_for(k):
        b, half = order[k // 2]
        return all(("rotate", b * HALVES + h, 1, 7) in out for h in range(half + 1) if b or h)

    for it in plan:
        out.append(it)
        while loads and split_for(loads[0]):
            out += [("load q", loads[0]), ("load k", loads.pop(0))]
        if it[0] != "score":
            continue
        due.append((seen + LAG, ("pv", seen)))
        if it[6]:
            if block + 2 < 2 * NCH:
                loads.append(block + 2)
            due.append((seen + LAG + 1, ("outputs", block)))
            block += 1
        while due and (due[0][0] <= seen or seen == total - 1):
            out.append(due.pop(0)[1])
        seen += 1
    return out + [("oT", NCH - 1, 1)]


def build(nc, x, qkv, wo, w_gate, w_up, w_down, cos_t, sin_t, out, stacks):
    plan = make_plan()
    slotted = [it for it in plan if it[0] in ("weights", "xT", "q", "k", "v", "ffnw", "score", "oT", "onT", "proj", "x1T",
                                              "gate", "up", "down")]
    others = [it for it in slotted if it[0] != "score" and not (it[0] in ("xT", "q", "k") and it[1] == 0)]
    early = [it for it in others if slotted.index(it) < [i[0] for i in slotted].index("score")]
    taking_turns = others[len(early):]
    side_items = [it for it in others if it not in taking_turns]
    ring = [it for it in slotted if it[0] == "score" or it in taking_turns]
    scores = [it for it in plan if it[0] == "score"]
    units = {half: group_units(half) for half in range(HALVES)}
    blocks = []
    for it in scores:
        if it[1:4] not in blocks:
            blocks.append(it[1:4])
    by_act = [it for it in slotted if it[0] in ("xT", "v", "ffnw", "onT", "x1T", "gate", "up")
              or (it[0] in ("q", "k") and it[1] > 0)]
    by_dve = [it for it in slotted if it[0] in ("weights", "oT", "proj", "down")]

    with ExitStack() as ctx:
        def sb(name, shape, dt=F32):
            return ctx.enter_context(nc.sbuf_tensor(name, shape, dt))

        def sem(name):
            return ctx.enter_context(nc.semaphore(name))

        slots = [ctx.enter_context(nc.psum_tensor(f"slot{i}", [P, 2, C], F32)) for i in range(3)]
        o_acc = ctx.enter_context(nc.psum_tensor("o_acc", [P, C], F32))
        side = ctx.enter_context(nc.psum_tensor("side", [P, C], F32))
        banks = [slots[i // 2][:, i % 2] for i in range(RING - 1)] + [side[:]]

        ident = sb("ident", [P, P])
        ident_bf = sb("ident_bf", [P, P], BF16)
        future = sb("future", [P, P], BF16)
        x_sb = sb("x_sb", [P, B * NT, P])
        xT = sb("xT", [P, 2, C])
        w_qkv = sb("w_qkv", [P, 3, P])
        w_o = sb("w_o", [P, P])
        w_ffn_i = sb("w_ffn_i", [P, 3, HID], I32)
        w_ffn = w_ffn_i[:].bitcast(F32)
        wT = sb("wT", [P, 3, P])
        woT = sb("woT", [P, P])
        ffT = sb("ffT", [P, 3, HID])
        cos_sb = sb("cos_sb", [P, S])
        sin_sb = sb("sin_sb", [P, S])
        raw = sb("raw", [P, 2, C])
        rots = [sb(f"rot{i}", [P, 2, C]) for i in range(2)]
        qk = sb("qk", [P, 2, C])
        parts = sb("parts", [P, 2, 3, C], BF16)
        qs = sb("qs", [ROWS, 2, SH, C], BF16)
        ks = sb("ks", [ROWS, SETS, HALVES, SH, C], BF16)
        vs = sb("vs", [P, B * NT, SETS * 4, GROUPS, 32])
        p_sb = sb("p_sb", [P, NP, C])
        o_sb = sb("o_sb", [P, SETS, C])
        den_inv = sb("den_inv", [P, NCH * SETS, CT * 4, GROUPS])
        o_rows = sb("o_rows", [P, CT, SETS, 64])
        o_n = sb("o_n", [P, C])
        y = sb("y", [P, 2, CT, P])
        x1T = sb("x1T", [P, C])
        st6 = sb("st6", [P, CT, 6])
        mv = sb("mv", [P, CT, 2])
        minus_half = sb("minus_half", [P, CT])
        ve = sb("ve", [P, CT])
        rstd = sb("rstd", [P, CT])
        gu = sb("gu", [P, 2, 2, C])
        eg = sb("eg", [P, 2, C])
        hT = sb("hT", [P, NHC, C])
        in_range = sb("in_range", [P, NCH * SETS * CT * 4 * GROUPS])
        v_square = sb("v_square", [P, C // GROUPS])
        v_sum = sb("v_sum", [P, NCH * GROUPS])
        v_small = sb("v_small", [P, NCH * GROUPS])
        fast_ok = sb("fast_ok", [P, 4])
        flag = sb("flag", [1, 1], I32)

        x_loaded = [sem(f"x_loaded{c}") for c in range(NCH)]
        w_qkv_loaded = sem("w_qkv_loaded")
        w_o_loaded = sem("w_o_loaded")
        w_ffn_loaded = sem("w_ffn_loaded")
        rope_loaded = sem("rope_loaded")
        ident_ready = sem("ident_ready")
        vs_preset = sem("vs_preset")
        ffn_dequantised = sem("ffn_dequantised")
        product_ready = sem("product_ready")
        act_emptied = sem("act_emptied")
        dve_emptied = sem("dve_emptied")
        exp_done = sem("exp_done")
        zeros_masked = sem("zeros_masked")
        pv_done = sem("pv_done")
        o_copied = sem("o_copied")
        part_ready = [sem("q_part_ready"), sem("k_part_ready")]
        v_checked = sem("v_checked")
        fast_ok_ready = sem("fast_ok_ready")
        fast_ok_across = sem("fast_ok_across")
        flag_ready = sem("flag_ready")
        mask_ready = sem("mask_ready")
        stacks_fetched = sem("stacks_fetched")
        scored = sem("scored")
        maximum_ready = sem("maximum_ready")
        exponentiated = sem("exponentiated")
        probs_ready = sem("probs_ready")
        transposed = sem("transposed")
        keys_first = sem("keys_first")
        summed = sem("summed")
        head_done = sem("head_done")
        tile_products = sem("tile_products")
        tile_copies = sem("tile_copies")
        tile_rows = sem("tile_rows")
        tile_rstd = sem("tile_rstd")
        tile_written = sem("tile_written")
        stack_written = [[sem(f"stack_written_{t}{c}") for t in "qk"] for c in range(NCH)]
        stacks_loaded = [sem(f"stacks_loaded{k}") for k in range(len(blocks))]
        dve_chain = sem("dve_chain")
        pool_chain = sem("pool_chain")
        stats_ready = sem("stats_ready")
        rstd_ready = sem("rstd_ready")
        rows_normalised = [sem("rows_normalised0"), sem("rows_normalised1")]
        hidden_ready = sem("hidden_ready")
        end_product = sem("end_product")
        end_copied = sem("end_copied")
        end_rows = sem("end_rows")
        end_rstd = sem("end_rstd")
        out_written = [sem(f"out_written{i}") for i in range(2)]

        block = ctx.enter_context(nc.Block())

        def number(items, it):
            return items.index(it) + 1

        def home(it):
            if it[0] == "score":
                return banks[ring.index(it) % RING]
            if it in side_items:
                return side
            if it in taking_turns:
                return banks[ring.index(it) % RING]
            return {"q": slots[0][:, 0], "k": slots[0][:, 1], "xT": slots[1][:, 0]}[it[0]]

        wide = [p_sb[:, 2 * i:2 * i + 2].rearrange("p a c -> p (a c)") for i in range(NP // 2)]
        masked, keep, probs, probsT, low = wide[0], wide[1], wide[2], wide[3], wide[6]
        causal = p_sb[:, 8:12].rearrange("p n c -> p (n c)")
        v_head = wide[7][:, 0:NT * DH].rearrange("p (t d) -> p t d", d=DH)
        attn_rows, attnT = wide[7][:, P:2 * P], wide[7][:, 2 * P:3 * P]
        top, shift, den, inv = (wide[7][:, 3 * P + i:3 * P + i + 1] for i in range(4))
        row, row_T = y[:, 0, 0], y[:, 0, 1]
        row_eg, row_h = gu[:, 0, 0, 0:HID], gu[:, 0, 1, 0:HID]

        def flag_of(eng):
            eng.wait_ge(flag_ready, 1)
            return eng.value_load(flag[0:1, 0:1], min_val=0, max_val=1)

        def careful(eng, head_work, tile_work):
            with eng.Fori(0, B) as b:
                with eng.Fori(0, HALVES) as half:
                    with eng.Fori(0, CT) as t:
                        tiles = b * NT + half * CT + t
                        with eng.Fori(0, HEADS // 2) as pair:
                            with eng.Fori(0, 2) as g:
                                head_work(b, half, t, pair, g, tiles * HEADS + pair * 2 + g)
                        tile_work(tiles)

        HALF = C // 2
        END_PE = ([(k, i) for k in ("onT", "proj", "x1T") for i in range(2)]
                  + [(k, i, wide) for i in range(2) for wide in range(2) for k in ("gate", "up")]
                  + [("down", i) for i in range(2)])
        END_ACT = [(k, i) for k in ("o_n", "x1T") for i in range(2)] + [("tanh", i, w) for i in range(2) for w in range(2)]
        END_DVE = ([(k, i) for k in ("stats 0", "scale 0") for i in range(2)]
                   + [("hidden", i, w) for i in range(2) for w in range(2)]
                   + [(k, i) for k in ("stats 1", "scale 1") for i in range(2)])
        end_banks = [[slots[n][:, i, 0:HALF] for i in range(2)] for n in range(3)]
        end_cols = [slice(i * HALF, (i + 1) * HALF) for i in range(2)]
        end_tiles = [slice((NCH - 1) * CT + 2 * i, (NCH - 1) * CT + 2 * i + 2) for i in range(2)]

        def end_hidden(i, wide):
            if wide == 0:
                return o_acc[:], side[:], eg[:, i], hT[:, 0:2, end_cols[i]]
            return end_banks[0][i], end_banks[1][i], gu[:, i, 0, 0:HALF], hT[:, 2:3, end_cols[i]]

        def last_product(k):
            return number(slotted, [i for i in scores if i[1:4] == blocks[k]][-1])

        def wait_product(eng, it):
            eng.wait_ge(product_ready, number(slotted, it))

        def wait_emptied(eng, it):
            if it[0] == "score":
                eng.wait_ge(zeros_masked, number(scores, it))
            elif it in by_act:
                eng.wait_ge(act_emptied, number(by_act, it))
            else:
                eng.wait_ge(dve_emptied, number(by_dve, it))

        chunk_rows = x.rearrange("b (c t p) d -> (b c) p t d", c=HALVES, p=P)
        out_rows = out.rearrange("b (c t p) d -> (b c) p t d", c=HALVES, p=P)

        def key_halves(k):
            b, half, st = blocks[k]
            had = {h for bb, h, ss in blocks[:k] if (bb, ss) == (b, st)}
            return [h for h in range(half + 1) if not had or h > max(had)]

        @block.sync
        def _(sp):
            sp.dma_start(w_qkv[:], qkv.rearrange("(t p) d -> p t d", p=P)).then_inc(w_qkv_loaded, 16)
            sp.dma_start(w_o[:], wo).then_inc(w_o_loaded, 16)
            sp.dma_start(cos_sb[:], cos_t).then_inc(rope_loaded, 16)
            sp.dma_start(sin_sb[:], sin_t).then_inc(rope_loaded, 16)
            sp.dma_start(x_sb[:, CT:2 * CT, :], chunk_rows[1]).then_inc(x_loaded[1], 16)
            for c in range(2, NCH):
                sp.dma_start(x_sb[:, c * CT:(c + 1) * CT, :], chunk_rows[c]).then_inc(x_loaded[c], 16)
            for n, w in enumerate((w_gate, w_up)):
                sp.dma_start(w_ffn_i[:, n, :].rearrange("p (t d) -> p t d", t=NHC),
                             w.rearrange("(t p) d -> p t d", p=P)).then_inc(w_ffn_loaded, 16)
            sp.dma_start(w_ffn_i[:, 2, :], w_down).then_inc(w_ffn_loaded, 16)
            for it in plan:
                if it[0] in ("q", "k") and it[1] == 0 or it[0] == "rotate" and it[3] == 7:
                    c = it[1]
                    n = it[2] if it[0] == "rotate" else "qk".index(it[0])
                    for part in range(3):
                        sp.wait_ge(part_ready[n], 3 * c + part + 1)
                        sp.dma_start(stacks[c, n, part], parts[:, n, part]).then_inc(stack_written[c][n], 16)
                if it[0] in ("load q", "load k"):
                    k = it[1]
                    b, half, st = blocks[k]
                    if k >= 2:
                        sp.wait_ge(product_ready, last_product(k - 2))
                    mine = slice(st * SH * C, (st + 1) * SH * C)
                if it[0] == "load k":
                    for h in key_halves(k):
                        c = b * HALVES + h
                        sp.wait_ge(stack_written[c][1], 3 * 16)
                        src = stacks[c, 1].rearrange("t (d h) s -> (t d) (h s)", d=DH)[:, mine]
                        sp.dma_start(ks[:, st, h].rearrange("p h s -> p (h s)"),
                                     src.unsqueeze(0).to_broadcast([3, 3 * DH, SH * C])).then_inc(stacks_loaded[k], 16)
                if it[0] == "load q":
                    c = b * HALVES + half
                    sp.wait_ge(stack_written[c][0], 3 * 16)
                    for part in range(3):
                        src = stacks[c, 0, part].rearrange("(d h) s -> d (h s)", d=DH)[:, mine]
                        sp.dma_start(qs[3 * DH * part:3 * DH * (part + 1), k % 2].rearrange("p h s -> p (h s)"),
                                     src.unsqueeze(0).to_broadcast([3, DH, SH * C])).then_inc(stacks_loaded[k], 16)
                if it[0] == "scale" and it[2] == 1:
                    e = it[1]
                    sp.wait_ge(rows_normalised[1], e + 1)
                    sp.dma_start(out_rows[it[1]], y[:, e % 2]).then_inc(out_written[e % 2], 16)
            for i in range(2):
                sp.wait_ge(end_rows, number(END_DVE, ("scale 1", i)))
                sp.dma_start(out_rows[NCH - 1][:, 2 * i:2 * i + 2], y[:, 1, 2 * i:2 * i + 2]).then_inc(out_written[1], 16)
            ok = flag_of(sp)
            sp.wait_ge(out_written[0], 2 * 16)
            sp.wait_ge(out_written[1], 3 * 16)

            def fetch(b, half, t, pair, g, n):
                sp.wait_ge(head_done, n + 1)
                for h in range(HALVES):
                    src = stacks[bass.ds(b * HALVES + h, 1), 1].rearrange("o t (d h) s -> h (o t d) s", d=DH)
                    src = src[bass.ds(pair * 2 + g, 1)].to_broadcast([3, 3 * DH, C])
                    sp.dma_start(ks[:, 0, 0, h], src).then_inc(stacks_fetched, 16)
                for part in range(3):
                    src = stacks[bass.ds(b * HALVES + half, 1), 0, part].rearrange("o (d h) s -> h (o d) s", d=DH)
                    src = src[bass.ds(pair * 2 + g, 1), :, bass.ds(t * P, P)].to_broadcast([3, DH, P])
                    sp.dma_start(qs[3 * DH * part:3 * DH * (part + 1), 0, 0, 0:P], src).then_inc(stacks_fetched, 16)

            def send(tiles):
                sp.wait_ge(tile_rows, 5 * tiles + 5)
                sp.dma_start(out.rearrange("b s d -> (b s) d")[bass.ds(tiles * P, P)], row).then_inc(tile_written, 16)

            with sp.If(ok == 0):
                careful(sp, fetch, send)
                sp.wait_ge(tile_written, 16 + 16 * B * NT)

        def rotate_step(eng, nce, link, c, n, src, step):
            cs = slice(c % HALVES * C, (c % HALVES + 1) * C)
            rot = rots[(c, n) in ROTATED_BY_DVE]
            if step == 0:
                before = [(a, b) for a in range(NCH) for b in range(2)
                          if (a, b) < (c, n) and ((a, b) in ROTATED_BY_DVE) == ((c, n) in ROTATED_BY_DVE)]
                if before:
                    eng.wait_ge(part_ready[before[-1][1]], 3 * before[-1][0] + 3)
                link(nce.tensor_tensor(rot[:, 0], src[:], cos_sb[:, cs], ALU.mult))
            elif step in (1, 2):
                lo, hi = ((0, 64), (64, 0))[step - 1]
                link(nce.tensor_tensor(rot[lo:lo + 64, 1], src[hi:hi + 64], sin_sb[hi:hi + 64, cs], ALU.mult))
            elif step == 3:
                if c > 0:
                    eng.wait_ge(part_ready[n], 3 * c)
                link(nce.tensor_tensor(qk[:, n], rot[:, 0], rot[:, 1], ALU.add))
            elif step == 4:
                if c > 0:
                    eng.wait_ge(stack_written[c - 1][n], 3 * 16)
                nce.tensor_copy(parts[:, n, 0], qk[:, n]).then_inc(part_ready[n], 1)
            elif step == 5:
                eng.wait_ge(part_ready[n], 3 * c + 1)
                link(nce.tensor_tensor(rot[:, 0], qk[:, n], parts[:, n, 0], ALU.subtract))
            elif step == 6:
                nce.tensor_copy(parts[:, n, 1], rot[:, 0]).then_inc(part_ready[n], 1)
            else:
                eng.wait_ge(part_ready[n], 3 * c + 2)
                nce.tensor_tensor(parts[:, n, 2], rot[:, 0], parts[:, n, 1], ALU.subtract).then_inc(part_ready[n], 1)

        @block.gpsimd
        def _(pool):
            chain = [0]

            def link(ins):
                chain[0] += 1
                ins.then_inc(pool_chain, 1)
                pool.wait_ge(pool_chain, chain[0])

            link(nc.gpsimd.memset(ident[:], 0.0))
            nc.gpsimd.affine_select(out=ident[:], in_=ident[:], compare_op=ALU.not_equal, fill=1.0, base=0,
                                    pattern=[[-1, P]], channel_multiplier=1).then_inc(ident_ready, 1)
            pool.wait_ge(ident_ready, 1)
            nc.gpsimd.tensor_copy(ident_bf[:], ident[:])
            link(nc.gpsimd.memset(future[:], 0.0))
            nc.gpsimd.affine_select(out=future[:], in_=future[:], compare_op=ALU.is_ge, fill=-1e30, base=0,
                                    pattern=[[1, P]], channel_multiplier=-1).then_inc(ident_ready, 1)
            link(nc.gpsimd.memset(vs[:, 0:CT], 0.0))
            for g in range(GROUPS):
                last = nc.gpsimd.memset(vs[:, 0:CT, :, g, 16 + 8 * g:24 + 8 * g], 1.0)
            last.then_inc(vs_preset, 1)
            link(nc.gpsimd.memset(vs[:, CT:B * NT], 0.0))
            for g in range(GROUPS):
                last = nc.gpsimd.memset(vs[:, CT:B * NT, :, g, 16 + 8 * g:24 + 8 * g], 1.0)
            last.then_inc(vs_preset, 1)
            link(nc.gpsimd.memset(minus_half[:], -0.5))
            pool.wait_ge(w_ffn_loaded, 48)
            nc.gpsimd.tensor_scalar(w_ffn, w_ffn_i[:], DEQUANT, None, ALU.mult).then_inc(ffn_dequantised, 1)

            done = {"rstd": 0, "scaled": 0, "hidden": 0}
            for it in plan:
                kind = it[0]
                if kind == "rotate" and it[1:3] not in ROTATED_BY_DVE:
                    _, c, n, step = it
                    if step == 0:
                        pool.wait_ge(act_emptied, number(by_act, ("qk"[n], c)))
                    if step in (1, 2):
                        if done["rstd"]:
                            pool.wait_ge(rstd_ready, done["rstd"])
                        if done["scaled"]:
                            pool.wait_ge(rows_normalised[1], done["scaled"])
                        if done["hidden"]:
                            pool.wait_ge(hidden_ready, done["hidden"])
                    rotate_step(pool, nc.gpsimd, link, c, n, raw[:, n], step)
                elif kind == "stats":
                    n = 2 * it[1] + it[2]
                    pool.wait_ge(stats_ready, n + 1)
                    nc.gpsimd.tensor_tensor(rstd[:], ve[:], minus_half[:], ALU.pow).then_inc(rstd_ready, 1)
                    done["rstd"] += 1
                elif kind == "scale" and it[2] == 1:
                    e = it[1]
                    pool.wait_ge(rstd_ready, 2 * e + 2)
                    for t in range(CT):
                        last = nc.gpsimd.tensor_scalar(y[:, e % 2, t], y[:, e % 2, t], mv[:, t, 0:1], rstd[:, t:t + 1],
                                                       ALU.subtract, ALU.mult)
                    last.then_inc(rows_normalised[1], 1)
                    done["scaled"] += 1
                elif kind == "gate":
                    m = (3 * it[1] + it[2]) % 2
                    pool.wait_ge(act_emptied, number(by_act, it))
                    link(nc.gpsimd.tensor_scalar(eg[:, m], eg[:, m], 1.0, 0.5, ALU.add, ALU.mult))
                    link(nc.gpsimd.tensor_tensor(eg[:, m], gu[:, m, 0], eg[:, m], ALU.mult))
                elif kind == "up":
                    e, hc = it[1], it[2]
                    m = (3 * e + hc) % 2
                    pool.wait_ge(act_emptied, number(by_act, it))
                    if e:
                        pool.wait_ge(product_ready, number(slotted, ("down", e - 1)))
                    nc.gpsimd.tensor_tensor(hT[:, hc], gu[:, m, 1], eg[:, m], ALU.mult).then_inc(hidden_ready, 1)
                    done["hidden"] += 1

            for n in range(4):
                pool.wait_ge(end_rows, number(END_DVE, (("stats 0", "stats 1")[n // 2], n % 2)))
                ts = slice(n % 2 * 2, n % 2 * 2 + 2)
                nc.gpsimd.tensor_tensor(rstd[:, ts], ve[:, ts], minus_half[:, ts], ALU.pow).then_inc(end_rstd, 1)

            with pool.If(flag_of(pool) == 0):
                pool.wait_ge(end_rows, len(END_DVE))
                nc.gpsimd.memset(causal[:], 1.0).then_inc(mask_ready, 1)
                pool.wait_ge(mask_ready, 1)
                nc.gpsimd.affine_select(out=causal[:], in_=causal[:], compare_op=ALU.is_ge, fill=0.0,
                                        base=(NT - 1) * P, pattern=[[-1, 2 * S]],
                                        channel_multiplier=1).then_inc(mask_ready, 1)
                with pool.Fori(0, B * NT) as tiles:
                    for half in range(2):
                        pool.wait_ge(tile_rows, 5 * tiles + (1, 4)[half])
                        nc.gpsimd.tensor_tensor(rstd[:, 0:1], ve[:, 0:1], minus_half[:, 0:1],
                                                ALU.pow).then_inc(tile_rstd, 1)

        @block.scalar
        def _(act):
            act.dma_start(x_sb[:, 0:CT, :], chunk_rows[0]).then_inc(x_loaded[0], 16)
            for it in plan:
                kind = it[0]
                if it in by_act:
                    wait_product(act, it)
                if kind == "xT":
                    if it[1] >= 2:
                        wait_product(act, ("v", it[1] - 2))
                    nc.scalar.activation(xT[:, it[1] % 2], home(it)[:], ACT.Copy).then_inc(act_emptied, 1)
                elif kind in ("q", "k") and it[1] > 0:
                    if it[1] > 1:
                        act.wait_ge(part_ready["qk".index(kind)], 3 * it[1])
                    nc.scalar.activation(raw[:, "qk".index(kind)], home(it)[:], ACT.Copy).then_inc(act_emptied, 1)
                elif kind == "v":
                    c = it[1]
                    act.wait_ge(vs_preset, 1 if c == 0 else 2)
                    src = home(it)[:].rearrange("p (t j g d) -> p t j g d", t=CT, g=GROUPS, d=DH)
                    for g in range(GROUPS):
                        last = nc.scalar.activation(vs[:, c * CT:(c + 1) * CT, :, g, 8 * g:8 * g + 8],
                                                    src[:, :, :, g, :], ACT.Copy)
                    last.then_inc(act_emptied, 1)
                    act.wait_ge(act_emptied, number(by_act, it))
                    for g in range(GROUPS):
                        last = nc.scalar.activation(v_square[:].rearrange("p (t j d) -> p t j d", t=CT, d=DH),
                                                    vs[:, c * CT:(c + 1) * CT, :, g, 8 * g:8 * g + 8], ACT.Square,
                                                    accum_out=v_sum[:, GROUPS * c + g:GROUPS * c + g + 1])
                        last.then_inc(v_checked, 1)
                        act.wait_ge(v_checked, GROUPS * c + g + 1)
                elif kind == "ffnw":
                    nc.scalar.activation(ffT[:, it[1]], home(it)[:, 0:HID], ACT.Copy).then_inc(act_emptied, 1)
                elif kind == "score":
                    u = scores.index(it)
                    wait_product(act, it)
                    if u >= NP:
                        act.wait_ge(pv_done, u - NP + 1)
                    nc.scalar.activation(p_sb[:, u % NP], home(it), ACT.Exp,
                                         scale=SCORE_SCALE).then_inc(exp_done, 1)
                elif kind == "outputs":
                    k = it[1]
                    last_unit = max(u for u, i in enumerate(scores) if i[1:4] == blocks[k])
                    act.wait_ge(pv_done, last_unit + 1)
                    if k >= 2:
                        wait_product(act, ("oT", k // 2 - 1, k % 2))
                    nc.scalar.activation(o_sb[:, k % 2], o_acc[:], ACT.Copy).then_inc(o_copied, 1)
                elif kind == "onT":
                    e = it[1]
                    if e:
                        wait_product(act, ("proj", e - 1))
                    nc.scalar.activation(o_n[:], home(it)[:], ACT.Copy).then_inc(act_emptied, 1)
                elif kind == "x1T":
                    e = it[1]
                    if e:
                        wait_product(act, ("up", e - 1, 2))
                    nc.scalar.activation(x1T[:], home(it)[:], ACT.Copy).then_inc(act_emptied, 1)
                elif kind == "gate":
                    n = 3 * it[1] + it[2]
                    if n >= 2:
                        act.wait_ge(hidden_ready, n - 1)
                    nc.scalar.activation(eg[:, n % 2], home(it)[:], ACT.Tanh, scale=0.5)
                    nc.scalar.activation(gu[:, n % 2, 0], home(it)[:], ACT.Copy).then_inc(act_emptied, 1)
                elif kind == "up":
                    n = 3 * it[1] + it[2]
                    nc.scalar.activation(gu[:, n % 2, 1], home(it)[:], ACT.Copy).then_inc(act_emptied, 1)

            for name, bank, to in (("onT", 0, o_n), ("x1T", 2, x1T)):
                for i in range(2):
                    act.wait_ge(end_product, number(END_PE, (name, i)))
                    nc.scalar.activation(to[:, end_cols[i]], end_banks[bank][i], ACT.Copy).then_inc(end_copied, 1)
            act.wait_ge(hidden_ready, 3 * (NCH - 1))
            for i in range(2):
                for wide in range(2):
                    act.wait_ge(end_product, number(END_PE, ("gate", i, wide)))
                    gate, _, tanh, _ = end_hidden(i, wide)
                    nc.scalar.activation(tanh, gate, ACT.Tanh, scale=0.5).then_inc(end_copied, 1)

            def head(b, half, t, pair, g, n):
                act.wait_ge(maximum_ready, n + 1)
                nc.scalar.activation(probs, masked, ACT.Exp, bias=shift, scale=SCORE_SCALE).then_inc(exponentiated, 1)
                act.wait_ge(transposed, n + 1)
                nc.scalar.activation(probsT, slots[1][:].rearrange("p a c -> p (a c)"),
                                     ACT.Copy).then_inc(keys_first, 1)

            def tile(tiles):
                act.wait_ge(tile_products, 5 * tiles + 1)
                nc.scalar.activation(attnT, side[:, 0:P], ACT.Copy).then_inc(tile_copies, 1)
                act.wait_ge(tile_products, 5 * tiles + 3)
                nc.scalar.activation(row_T, side[:, 0:P], ACT.Copy).then_inc(tile_copies, 1)
                act.wait_ge(tile_products, 5 * tiles + 4)
                nc.scalar.activation(row_eg, slots[0][:, 0, 0:HID], ACT.Tanh, scale=0.5).then_inc(tile_copies, 1)

            with act.If(flag_of(act) == 0):
                careful(act, head, tile)

        @block.vector
        def _(dve):
            chain = [0]

            def link(ins):
                chain[0] += 1
                ins.then_inc(dve_chain, 1)
                dve.wait_ge(dve_chain, chain[0])


            def end_stats(link, i):
                for t in (2 * i, 2 * i + 1):
                    last = nc.vector.bn_stats(st6[:, t], y[:, 1, t])
                link(last)
                for t in (2 * i, 2 * i + 1):
                    last = nc.vector.bn_aggr(mv[:, t], st6[:, t])
                link(last)
                return nc.vector.tensor_scalar(ve[:, 2 * i:2 * i + 2], mv[:, 2 * i:2 * i + 2, 1], EPS, None, ALU.add)

            scaled = [0]

            def end_scale():
                for i in range(2):
                    scaled[0] += 1
                    dve.wait_ge(end_rstd, scaled[0])
                    for t in (2 * i, 2 * i + 1):
                        last = nc.vector.tensor_scalar(y[:, 1, t], y[:, 1, t], mv[:, t, 0:1], rstd[:, t:t + 1],
                                                       ALU.subtract, ALU.mult)
                    last.then_inc(end_rows, 1)
            for it in plan:
                kind = it[0]
                if kind == "weights":
                    wait_product(dve, it)
                    for n in range(2):
                        nc.vector.tensor_copy(wT[:, n].rearrange("p (d h) -> p d h", d=DH),
                                              side[:, n * P:(n + 1) * P].rearrange("p (h d) -> p d h", d=DH))
                    nc.vector.tensor_copy(wT[:, 2], side[:, 2 * P:3 * P])
                    nc.vector.tensor_copy(woT[:], side[:, 3 * P:4 * P]).then_inc(dve_emptied, 1)
                elif kind in ("q", "k") and it[1] == 0:
                    wait_product(dve, it)
                    dve.wait_ge(rope_loaded, 32)
                    for step in range(8):
                        rotate_step(dve, nc.vector, link, 0, "qk".index(kind), home(it), step)
                elif kind == "rotate" and it[1:3] in ROTATED_BY_DVE:
                    _, c, n, step = it
                    if step == 0:
                        dve.wait_ge(act_emptied, number(by_act, ("qk"[n], c)))
                    rotate_step(dve, nc.vector, link, c, n, raw[:, n], step)
                elif kind == "score":
                    u = scores.index(it)
                    dve.wait_ge(exp_done, u + 1)
                    e = p_sb[:, u % NP]
                    nc.vector.scalar_tensor_tensor(out=e, in0=home(it),
                                                   scalar=0.0, in1=e, op0=ALU.not_equal,
                                                   op1=ALU.mult).then_inc(zeros_masked, 1)
                elif kind == "oT":
                    e, st = it[1], it[2]
                    wait_product(dve, it)
                    strips = home(it)[:].rearrange("p (t r) -> p t r", r=32)
                    mine = den_inv[:, SETS * e + st]
                    link(nc.vector.reciprocal(mine, strips[:, :, 16:32:8]))
                    if e:
                        wait_product(dve, ("onT", e - 1))
                    for g in range(GROUPS):
                        last = nc.vector.tensor_tensor(
                            o_rows[:, :, st].rearrange("p t (j g d) -> p t j g d", g=GROUPS, d=DH)[:, :, :, g],
                            strips[:, :, 8 * g:8 * g + 8].rearrange("p (t j) d -> p t j d", j=4),
                            mine[:, :, g:g + 1].rearrange("p (t j) o -> p t j o", j=4)
                            .to_broadcast([P, CT, 4, DH]), ALU.mult)
                    last.then_inc(dve_emptied, 1)
                elif kind in ("proj", "down"):
                    e = it[1]
                    wait_product(dve, it)
                    rows = y[:, e % 2].rearrange("p t d -> p (t d)")
                    if kind == "proj":
                        dve.wait_ge(x_loaded[it[1]], 16)
                        if e >= 2:
                            dve.wait_ge(out_written[e % 2], 16 * (e // 2))
                    other = x_sb[:, it[1] * CT:(it[1] + 1) * CT, :].rearrange("p t d -> p (t d)")
                    nc.vector.tensor_tensor(rows, home(it)[:], other if kind == "proj" else rows,
                                            ALU.add).then_inc(dve_emptied, 1)
                elif kind == "stats":
                    e, which = it[1], it[2]
                    dve.wait_ge(dve_emptied, number(by_dve, (("proj", "down")[which], it[1])))
                    if e or which:
                        dve.wait_ge(rows_normalised[1 - which], e + which)
                    for t in range(CT):
                        last = nc.vector.bn_stats(st6[:, t], y[:, e % 2, t])
                    link(last)
                    for t in range(CT):
                        last = nc.vector.bn_aggr(mv[:, t], st6[:, t])
                    link(last)
                    nc.vector.tensor_scalar(ve[:], mv[:, :, 1], EPS, None, ALU.add).then_inc(stats_ready, 1)
                elif kind == "scale" and it[2] == 0:
                    e = it[1]
                    dve.wait_ge(rstd_ready, 2 * e + 1)
                    for t in range(CT):
                        last = nc.vector.tensor_scalar(y[:, e % 2, t], y[:, e % 2, t], mv[:, t, 0:1], rstd[:, t:t + 1],
                                                       ALU.subtract, ALU.mult)
                    last.then_inc(rows_normalised[0], 1)

            for i in range(2):
                tiles, rows = end_tiles[i], y[:, 1, 2 * i:2 * i + 2]
                dve.wait_ge(end_product, number(END_PE, ("proj", i)))
                if i == 0:
                    dve.wait_ge(out_written[1], 16)
                    dve.wait_ge(rows_normalised[1], NCH - 1)
                link(nc.vector.tensor_tensor(rows, end_banks[1][i].rearrange("p (t d) -> p t d", d=P), x_sb[:, tiles],
                                             ALU.add))
                end_stats(link, i).then_inc(end_rows, 1)
            end_scale()
            dve.wait_ge(v_checked, NCH * GROUPS)
            inverses = den_inv[:].rearrange("p k a g -> p (k a g)")
            link(nc.vector.tensor_scalar(in_range[:], inverses, 1.0 / WINDOW, None, ALU.is_ge))
            link(nc.vector.scalar_tensor_tensor(out=in_range[:], in0=inverses, scalar=WINDOW, in1=in_range[:],
                                                op0=ALU.is_le, op1=ALU.mult))
            link(nc.vector.tensor_reduce(fast_ok[:, 0:1], in_range[:], AX_X, ALU.min))
            link(nc.vector.tensor_scalar(v_small[:], v_sum[:], V_LIMIT ** 2, None, ALU.is_le))
            link(nc.vector.tensor_reduce(fast_ok[:, 1:2], v_small[:], AX_X, ALU.min))
            nc.vector.tensor_tensor(fast_ok[:, 2:3], fast_ok[:, 0:1], fast_ok[:, 1:2], ALU.mult).then_inc(fast_ok_ready, 1)
            dve.wait_ge(fast_ok_across, 1)
            link(nc.vector.tensor_reduce(fast_ok[0:1, 3:4], slots[2][0:1, 0, C - P:C], AX_X, ALU.min))
            nc.vector.tensor_copy(flag[:], fast_ok[0:1, 3:4]).then_inc(flag_ready, 1)
            for i in range(2):
                for wide in range(2):
                    gate, up, tanh, h = end_hidden(i, wide)
                    dve.wait_ge(end_copied, number(END_ACT, ("tanh", i, wide)))
                    link(nc.vector.scalar_tensor_tensor(out=tanh, in0=tanh, scalar=1.0, in1=gate, op0=ALU.add,
                                                        op1=ALU.mult))
                    dve.wait_ge(end_product, number(END_PE, ("up", i, wide)))
                    nc.vector.scalar_tensor_tensor(out=h, in0=tanh.rearrange("p (n c) -> p n c", c=HALF), scalar=0.5,
                                                   in1=up.rearrange("p (n c) -> p n c", c=HALF), op0=ALU.mult,
                                                   op1=ALU.mult).then_inc(end_rows, 1)
            for i in range(2):
                rows = y[:, 1, 2 * i:2 * i + 2]
                dve.wait_ge(end_product, number(END_PE, ("down", i)))
                link(nc.vector.tensor_tensor(rows, end_banks[2][i].rearrange("p (t d) -> p t d", d=P), rows, ALU.add))
                end_stats(link, i).then_inc(end_rows, 1)
            end_scale()

            def head(b, half, t, pair, g, n):
                dve.wait_ge(scored, n + 1)
                s = slots[0][:].rearrange("p a c -> p (a c)")
                done = (NT - 1) * P - half * C - t * P
                nc.vector.scalar_tensor_tensor(out=keep, in0=s, scalar=0.0, in1=causal[:, bass.ds(done, S)],
                                               op0=ALU.not_equal, op1=ALU.mult)
                dve.drain()
                nc.vector.tensor_tensor(masked, s, keep, ALU.mult)
                nc.vector.tensor_scalar(low, keep, 1.0, 3e38, ALU.subtract, ALU.mult)
                dve.drain()
                nc.vector.tensor_tensor(masked, masked, low, ALU.add)
                dve.drain()
                nc.vector.tensor_reduce(top, masked, AX_X, ALU.max)
                dve.drain()
                nc.vector.tensor_scalar(shift, top, -SCORE_SCALE, None, ALU.mult).then_inc(maximum_ready, 1)
                nc.vector.tensor_copy(v_head, vs[:].rearrange("p t j g r -> p t j (g r)")
                                      [:, bass.ds(b * NT, NT), bass.ds(pair, 1), bass.ds(g * (32 + DH), DH)]
                                      .rearrange("p t o d -> p t (o d)"))
                dve.wait_ge(exponentiated, n + 1)
                nc.vector.tensor_tensor(probs, probs, keep, ALU.mult)
                dve.drain()
                nc.vector.tensor_reduce(den, probs, AX_X, ALU.add)
                dve.drain()
                nc.vector.reciprocal(inv, den).then_inc(probs_ready, 1)
                dve.wait_ge(summed, n + 1)
                nc.vector.tensor_scalar(attn_rows[:, bass.ds(pair * (2 * DH) + g * DH, DH)], o_acc[:, 0:DH], inv, None,
                                        ALU.mult).then_inc(head_done, 1)

            def norm_stats():
                dve.drain()
                nc.vector.bn_stats(st6[:, 0], row)
                dve.drain()
                nc.vector.bn_aggr(mv[:, 0], st6[:, 0])
                dve.drain()
                nc.vector.tensor_scalar(ve[:, 0:1], mv[:, 0, 1:2], EPS, None, ALU.add).then_inc(tile_rows, 1)

            def norm_scale():
                nc.vector.tensor_scalar(row, row, mv[:, 0, 0:1], rstd[:, 0:1], ALU.subtract,
                                        ALU.mult).then_inc(tile_rows, 1)

            def tile(tiles):
                dve.wait_ge(tile_written, 16 * tiles + 16)
                dve.wait_ge(tile_products, 5 * tiles + 2)
                nc.vector.tensor_tensor(row, side[:, P:2 * P],
                                        x_sb[:, bass.ds(tiles, 1)].rearrange("p o d -> p (o d)"), ALU.add)
                norm_stats()
                dve.wait_ge(tile_rstd, 2 * tiles + 1)
                norm_scale()
                dve.wait_ge(tile_copies, 3 * tiles + 3)
                nc.vector.tensor_scalar(row_eg, row_eg, 1.0, 0.5, ALU.add, ALU.mult)
                dve.drain()
                nc.vector.tensor_tensor(row_eg, slots[0][:, 0, 0:HID], row_eg, ALU.mult)
                dve.drain()
                nc.vector.tensor_tensor(row_h, slots[1][:, 0, 0:HID], row_eg, ALU.mult).then_inc(tile_rows, 1)
                dve.wait_ge(tile_products, 5 * tiles + 5)
                nc.vector.tensor_tensor(row, side[:, 0:P], row, ALU.add)
                norm_stats()
                dve.wait_ge(tile_rstd, 2 * tiles + 2)
                norm_scale()

            with dve.If(flag_of(dve) == 0):
                dve.wait_ge(mask_ready, 2)
                nc.vector.memset(attnT, 0.0).then_inc(tile_written, 16)
                nc.vector.memset(attn_rows, 0.0).then_inc(head_done, 1)
                careful(dve, head, tile)

        @block.tensor
        def _(pe):
            def mm(o, lhsT, rhs, start=True, stop=True, **kw):
                return nc.tensor.matmul(o, lhsT, rhs, start=start, stop=stop, **kw)

            for it in plan:
                kind = it[0]
                if it in side_items[1:]:
                    wait_emptied(pe, side_items[side_items.index(it) - 1])
                if it == ring[RING - 1]:
                    wait_emptied(pe, early[-1])
                if it in ring[RING:]:
                    wait_emptied(pe, ring[ring.index(it) - RING])
                if kind == "weights":
                    pe.wait_ge(ident_ready, 1)
                    pe.wait_ge(w_qkv_loaded, 16)
                    for n in range(3):
                        nc.tensor.transpose(side[:, n * P:(n + 1) * P], w_qkv[:, n], ident[:])
                    pe.wait_ge(w_o_loaded, 16)
                    last = nc.tensor.transpose(side[:, 3 * P:4 * P], w_o[:], ident[:])
                elif kind == "xT":
                    c = it[1]
                    pe.wait_ge(x_loaded[c], 16)
                    for t in range(CT):
                        last = nc.tensor.transpose(home(it)[:, t * P:(t + 1) * P], x_sb[:, c * CT + t], ident[:])
                elif kind in ("q", "k"):
                    c, n = it[1], "qk".index(kind)
                    wait_emptied(pe, ("weights",))
                    pe.wait_ge(act_emptied, number(by_act, ("xT", c)))
                    last = mm(home(it)[:], wT[:, n], xT[:, c % 2])
                elif kind == "v":
                    c = it[1]
                    for t in range(CT):
                        last = mm(home(it)[:, t * P:(t + 1) * P], xT[:, c % 2, t * P:(t + 1) * P], wT[:, 2])
                elif kind == "ffnw":
                    pe.wait_ge(ffn_dequantised, 1)
                    for hc in range(NHC):
                        last = nc.tensor.transpose(home(it)[:, hc * P:(hc + 1) * P],
                                                   w_ffn[:, it[1], hc * P:(hc + 1) * P], ident[:])
                elif kind == "score":
                    _, b, half, st, g, n, _ = it
                    diag = units[half][n][1]
                    k, u = blocks.index((b, half, st)), scores.index(it)
                    if u == 0:
                        pe.wait_ge(ident_ready, 2)
                    pe.wait_ge(stacks_loaded[k], 16 * (3 + len(key_halves(k))))
                    for jp, jl, i, col, width, first in units[half][n][0]:
                        head = 4 * jp + 2 * jl + g
                        last = mm(home(it)[:, col:col + width],
                                  ks[:, st, i // CT, head, (i % CT) * P:(i % CT + 1) * P],
                                  qs[:, k % 2, head, first:first + width],
                                  start=col == 0, stop=not diag, skip_group_check=True)
                    if diag:
                        bank = home(it)
                        blocks_in = {"first": bank[:, 0:P].unsqueeze(1),
                                     "outer": bank.rearrange("p (a c) -> p a c", c=P)[:, 0:CT:CT - 1],
                                     "inner": bank.rearrange("p (a c) -> p a c", a=2)[:, :, 0:P]}[diag]
                        last = mm(blocks_in, ident_bf[:],
                                  future[:].unsqueeze(1).to_broadcast([P, blocks_in.shape[1], P]), start=False,
                                  skip_group_check=True)
                elif kind == "pv":
                    u = it[1]
                    _, b, half, st, g, n, block_ends = scores[u]
                    k = blocks.index((b, half, st))
                    pieces, diag, done = units[half][n]
                    if not done:
                        continue
                    pe.wait_ge(zeros_masked, u + 1)
                    if g == 0 and done[0] == 0:
                        pe.wait_ge(act_emptied, number(by_act, ("v", b * HALVES + half)))
                        if k:
                            pe.wait_ge(o_copied, k)
                    held = [(u + m, piece) for m in range(-3 if diag != "inner" else -1, 1)
                            for piece in units[half][n + m][0]]
                    for tile in done:
                        for v, (jp, jl, i, col, width, first) in held:
                            if i != tile:
                                continue
                            j = 2 * jp + jl
                            last = mm(o_acc[32 * j:32 * j + 32, first:first + width],
                                      vs[:, b * NT + i, 4 * st + j, g, :],
                                      p_sb[:, v % NP, col:col + width],
                                      start=(g == 0 and i == 0), stop=(block_ends and jp == 1 and jl == 1),
                                      skip_group_check=True)
                    last.then_inc(pv_done, 2 if diag == "inner" else 4)
                elif kind == "oT":
                    e, st = it[1], it[2]
                    pe.wait_ge(o_copied, 2 * e + st + 1)
                    for t in range(CT):
                        last = nc.tensor.transpose(home(it)[:, t * P:(t + 1) * P], o_sb[:, st, t * P:(t + 1) * P],
                                                   ident[:])
                elif kind == "onT":
                    wait_emptied(pe, ("oT", it[1], 1))
                    for t in range(CT):
                        last = nc.tensor.transpose(home(it)[:, t * P:(t + 1) * P],
                                                   o_rows[:, t].rearrange("p a r -> p (a r)"), ident[:])
                elif kind == "proj":
                    wait_emptied(pe, ("onT", it[1]))
                    for t in range(CT):
                        last = mm(home(it)[:, t * P:(t + 1) * P], o_n[:, t * P:(t + 1) * P], woT[:])
                elif kind == "x1T":
                    e = it[1]
                    pe.wait_ge(rows_normalised[0], e + 1)
                    for t in range(CT):
                        last = nc.tensor.transpose(home(it)[:, t * P:(t + 1) * P], y[:, e % 2, t], ident[:])
                elif kind in ("gate", "up"):
                    wait_emptied(pe, ("x1T", it[1]))
                    last = mm(home(it)[:], ffT[:, ("gate", "up").index(kind), it[2] * P:(it[2] + 1) * P], x1T[:])
                elif kind == "down":
                    e = it[1]
                    pe.wait_ge(hidden_ready, 3 * e + 3)
                    for t in range(CT):
                        for hc in range(NHC):
                            last = mm(home(it)[:, t * P:(t + 1) * P], hT[:, hc, t * P:(t + 1) * P],
                                      ffT[:, 2, hc * P:(hc + 1) * P], start=(hc == 0), stop=(hc == NHC - 1))
                if it in slotted:
                    last.then_inc(product_ready, 1)

            def end_transpose(bank, i, source):
                for t in range(2):
                    last = nc.tensor.transpose(end_banks[bank][i][:, t * P:(t + 1) * P], source(2 * i + t), ident[:])
                last.then_inc(end_product, 1)

            wait_emptied(pe, ("oT", NCH - 1, 1))
            for i in range(2):
                end_transpose(0, i, lambda t: o_rows[:, t].rearrange("p a r -> p (a r)"))
            for i in range(2):
                pe.wait_ge(end_copied, number(END_ACT, ("o_n", i)))
                for t in range(2):
                    last = mm(end_banks[1][i][:, t * P:(t + 1) * P], o_n[:, (2 * i + t) * P:(2 * i + t + 1) * P], woT[:])
                last.then_inc(end_product, 1)
            for i in range(2):
                pe.wait_ge(end_rows, number(END_DVE, ("scale 0", i)))
                end_transpose(2, i, lambda t: y[:, 1, t])
            for i in range(2):
                pe.wait_ge(end_copied, number(END_ACT, ("x1T", i)))
                for wide in range(2):
                    if (i, wide) == (1, 0):
                        pe.wait_ge(end_rows, number(END_DVE, ("hidden", 0, 0)))
                    for n in range(2):
                        bank = end_hidden(i, wide)[n]
                        for j, hc in enumerate(((0, 1), (2,))[wide]):
                            last = mm(bank[:, j * HALF:(j + 1) * HALF], ffT[:, n, hc * P:(hc + 1) * P], x1T[:, end_cols[i]])
                        last.then_inc(end_product, 1)
                    if (i, wide) == (0, 0):
                        pe.wait_ge(fast_ok_ready, 1)
                        mm(slots[2][0:1, 0, C - P:C], fast_ok[:, 2:3], ident[:]).then_inc(fast_ok_across, 1)
            for i in range(2):
                pe.wait_ge(end_rows, number(END_DVE, ("hidden", i, 1)))
                for t in range(2):
                    for hc in range(NHC):
                        last = mm(end_banks[2][i][:, t * P:(t + 1) * P], hT[:, hc, (2 * i + t) * P:(2 * i + t + 1) * P],
                                  ffT[:, 2, hc * P:(hc + 1) * P], start=hc == 0, stop=hc == NHC - 1)
                last.then_inc(end_product, 1)

            def head(b, half, t, pair, g, n):
                pe.wait_ge(stacks_fetched, 80 * n + 80)
                for h in range(HALVES):
                    last = mm(slots[0][:, h], qs[:, 0, 0, 0:P], ks[:, 0, 0, h])
                last.then_inc(scored, 1)
                pe.wait_ge(probs_ready, n + 1)
                for i in range(NT):
                    last = nc.tensor.transpose(slots[1][:, i // CT, (i % CT) * P:(i % CT + 1) * P],
                                               probs[:, i * P:(i + 1) * P], ident[:])
                last.then_inc(transposed, 1)
                pe.wait_ge(keys_first, n + 1)
                for i in range(NT):
                    last = mm(o_acc[:, 0:DH], probsT[:, i * P:(i + 1) * P], v_head[:, i], start=i == 0, stop=i == NT - 1)
                last.then_inc(summed, 1)

            def tile(tiles):
                pe.wait_ge(head_done, HEADS * tiles + HEADS + 1)
                nc.tensor.transpose(side[:, 0:P], attn_rows, ident[:]).then_inc(tile_products, 1)
                pe.wait_ge(tile_copies, 3 * tiles + 1)
                mm(side[:, P:2 * P], attnT, woT[:]).then_inc(tile_products, 1)
                pe.wait_ge(tile_rows, 5 * tiles + 2)
                nc.tensor.transpose(side[:, 0:P], row, ident[:]).then_inc(tile_products, 1)
                pe.wait_ge(tile_copies, 3 * tiles + 2)
                for n in range(2):
                    for hc in range(NHC):
                        cs = slice(hc * P, (hc + 1) * P)
                        last = mm(slots[n][:, 0, cs], ffT[:, n, cs], row_T)
                last.then_inc(tile_products, 1)
                pe.wait_ge(tile_rows, 5 * tiles + 3)
                for hc in range(NHC):
                    cs = slice(hc * P, (hc + 1) * P)
                    last = mm(side[:, 0:P], row_h[:, cs], ffT[:, 2, cs], start=hc == 0, stop=hc == NHC - 1)
                last.then_inc(tile_products, 1)

            with pe.If(flag_of(pe) == 0):
                careful(pe, head, tile)


_INS = ["L0_attn_x", "L0_attn_qkv", "L0_attn_wo", "L0_ffn_w_gate", "L0_ffn_w_up", "L0_ffn_w_down"]


def rope_tables():
    import numpy as np

    inv = (1.0 / np.float32(10000.0) ** (np.arange(0, DH, 2, dtype=np.float32) / np.float32(DH))).astype(np.float32)
    ang = np.arange(S, dtype=np.float32)[:, None] * inv[None, :]
    d = np.arange(P) // HEADS
    cos = np.cos(ang).astype(np.float32).T[d % (DH // 2)]
    sin = np.sin(ang).astype(np.float32).T[d % (DH // 2)]
    sin = np.where((d < DH // 2)[:, None], sin, -sin).astype(np.float32)
    return np.ascontiguousarray(cos), np.ascontiguousarray(sin)


def kernel(**inputs):
    import numpy as _np
    import concourse.bacc as _bacc
    from concourse import mybir as _mybir
    from concourse.bass_utils import run_bass_kernel_spmd as _run

    nc = _bacc.Bacc("TRN2", target_bir_lowering=False, num_devices=1)
    arrays, args = {}, []
    cos, sin = rope_tables()
    for name, a in [(n, inputs[n]) for n in _INS] + [("cos", cos), ("sin", sin)]:
        a = _np.ascontiguousarray(a)
        arrays[f"in_{name}_dram"] = a
        args.append(nc.dram_tensor(f"in_{name}_dram", a.shape, _mybir.dt.from_np(a.dtype), kind="ExternalInput").ap())
    args.append(nc.dram_tensor("out_0_dram", (B, S, D), F32, kind="ExternalOutput").ap())
    args.append(nc.dram_tensor("stacks_dram", (NCH, 2, 3, P, C), BF16, kind="Internal").ap())
    build(nc, *args)
    r = _run(nc, [arrays], core_ids=[0])
    return r.results[0]["out_0_dram"]
```
